# Optimizing a Trainium2 kernel written in Bass

```python
import numpy as np
import jax
import jax.numpy as jnp

def _softmax(x, axis=-1):
    return jax.nn.softmax(x, axis=axis)

def _gelu(x):
    return jax.nn.gelu(x, approximate=True)

def _silu(x):
    return jax.nn.silu(x)

def _sigmoid(x):
    return jax.nn.sigmoid(x)

def _layernorm(x, axis=-1, eps=1e-05):
    m = jnp.mean(x, axis=axis, keepdims=True)
    v = jnp.var(x, axis=axis, keepdims=True)
    return (x - m) / jnp.sqrt(v + eps)

def _scatter_add(tgt, idx, src, axis=0):
    return tgt.at[idx].add(src)

def _segment_sum(src, seg, n):
    return jax.ops.segment_sum(src, seg, n)
kernel_name = 'mk_dlrm_tower_d1_rec_r8_b34b01'

def setup_inputs(seed: int=0):
    np.random.seed(seed)
    _w = jnp.asarray

    def _rec_inputs():
        import jax
        import jax.numpy as jnp
        _tk = jax.random.key(seed)
        ids = jnp.stack([jax.random.randint(jax.random.fold_in(_tk, 200 + f), (2048,), 0, v, jnp.int32) for f, v in enumerate([1000, 1000, 1000, 125000, 12500, 12500, 12500, 1000, 12500, 12500, 1000, 125000, 125000, 12500, 12500, 1000, 1250, 12500, 1000, 1000, 1250, 1000, 1000, 1250, 1000, 1250])], axis=1)
        tbl_0 = 0.05 * jax.random.normal(jax.random.fold_in(_tk, 500 + 0), (1000, 64), jnp.float32)
        tbl_1 = 0.05 * jax.random.normal(jax.random.fold_in(_tk, 500 + 1), (1000, 64), jnp.float32)
        tbl_2 = 0.05 * jax.random.normal(jax.random.fold_in(_tk, 500 + 2), (1000, 64), jnp.float32)
        tbl_3 = 0.05 * jax.random.normal(jax.random.fold_in(_tk, 500 + 3), (125000, 64), jnp.float32)
        tbl_4 = 0.05 * jax.random.normal(jax.random.fold_in(_tk, 500 + 4), (12500, 64), jnp.float32)
        tbl_5 = 0.05 * jax.random.normal(jax.random.fold_in(_tk, 500 + 5), (12500, 64), jnp.float32)
        tbl_6 = 0.05 * jax.random.normal(jax.random.fold_in(_tk, 500 + 6), (12500, 64), jnp.float32)
        tbl_7 = 0.05 * jax.random.normal(jax.random.fold_in(_tk, 500 + 7), (1000, 64), jnp.float32)
        tbl_8 = 0.05 * jax.random.normal(jax.random.fold_in(_tk, 500 + 8), (12500, 64), jnp.float32)
        tbl_9 = 0.05 * jax.random.normal(jax.random.fold_in(_tk, 500 + 9), (12500, 64), jnp.float32)
        tbl_10 = 0.05 * jax.random.normal(jax.random.fold_in(_tk, 500 + 10), (1000, 64), jnp.float32)
        tbl_11 = 0.05 * jax.random.normal(jax.random.fold_in(_tk, 500 + 11), (125000, 64), jnp.float32)
        tbl_12 = 0.05 * jax.random.normal(jax.random.fold_in(_tk, 500 + 12), (125000, 64), jnp.float32)
        tbl_13 = 0.05 * jax.random.normal(jax.random.fold_in(_tk, 500 + 13), (12500, 64), jnp.float32)
        tbl_14 = 0.05 * jax.random.normal(jax.random.fold_in(_tk, 500 + 14), (12500, 64), jnp.float32)
        tbl_15 = 0.05 * jax.random.normal(jax.random.fold_in(_tk, 500 + 15), (1000, 64), jnp.float32)
        tbl_16 = 0.05 * jax.random.normal(jax.random.fold_in(_tk, 500 + 16), (1250, 64), jnp.float32)
        tbl_17 = 0.05 * jax.random.normal(jax.random.fold_in(_tk, 500 + 17), (12500, 64), jnp.float32)
        tbl_18 = 0.05 * jax.random.normal(jax.random.fold_in(_tk, 500 + 18), (1000, 64), jnp.float32)
        tbl_19 = 0.05 * jax.random.normal(jax.random.fold_in(_tk, 500 + 19), (1000, 64), jnp.float32)
        tbl_20 = 0.05 * jax.random.normal(jax.random.fold_in(_tk, 500 + 20), (1250, 64), jnp.float32)
        tbl_21 = 0.05 * jax.random.normal(jax.random.fold_in(_tk, 500 + 21), (1000, 64), jnp.float32)
        tbl_22 = 0.05 * jax.random.normal(jax.random.fold_in(_tk, 500 + 22), (1000, 64), jnp.float32)
        tbl_23 = 0.05 * jax.random.normal(jax.random.fold_in(_tk, 500 + 23), (1250, 64), jnp.float32)
        tbl_24 = 0.05 * jax.random.normal(jax.random.fold_in(_tk, 500 + 24), (1000, 64), jnp.float32)
        tbl_25 = 0.05 * jax.random.normal(jax.random.fold_in(_tk, 500 + 25), (1250, 64), jnp.float32)
        _rk = jax.random.fold_in(_tk, 7)
        r_dense_t = 7.22013e-05 + 1.00017 * jax.random.normal(jax.random.fold_in(_rk, 101), (2048, 256), jnp.float32)
        W_top1 = 0.0360844 * jax.random.normal(jax.random.fold_in(_tk, 801), (768, 512), jnp.float32)
        W_top2 = 0.0441942 * jax.random.normal(jax.random.fold_in(_tk, 802), (512, 256), jnp.float32)
        W_top3 = 0.0625 * jax.random.normal(jax.random.fold_in(_tk, 803), (256, 1), jnp.float32)
        b_top1 = jnp.zeros((512,), jnp.float32)
        b_top2 = jnp.zeros((256,), jnp.float32)
        return (r_dense_t, ids, tbl_0, tbl_1, tbl_2, tbl_3, tbl_4, tbl_5, tbl_6, tbl_7, tbl_8, tbl_9, tbl_10, tbl_11, tbl_12, tbl_13, tbl_14, tbl_15, tbl_16, tbl_17, tbl_18, tbl_19, tbl_20, tbl_21, tbl_22, tbl_23, tbl_24, tbl_25, W_top1, b_top1, W_top2, b_top2, W_top3)
    r_dense_t, ids, tbl_0, tbl_1, tbl_2, tbl_3, tbl_4, tbl_5, tbl_6, tbl_7, tbl_8, tbl_9, tbl_10, tbl_11, tbl_12, tbl_13, tbl_14, tbl_15, tbl_16, tbl_17, tbl_18, tbl_19, tbl_20, tbl_21, tbl_22, tbl_23, tbl_24, tbl_25, W_top1, b_top1, W_top2, b_top2, W_top3 = _rec_inputs()

    def _L0_rec_setup():
        import jax, jax.numpy as jnp
        import numpy as np
        EPS = 1e-05
        NI = 33
        TRIL_I, TRIL_J = np.tril_indices(NI, k=-1)

        def layer_norm(x, g, b):
            m = jnp.mean(x, axis=-1, keepdims=True)
            v = jnp.mean(jnp.square(x - m), axis=-1, keepdims=True)
            return (x - m) * jax.lax.rsqrt(v + EPS) * g + b
        key = jax.random.key(seed)
        ks = jax.random.split(key, 8)
        B, D_DENSE, N_SP, D_SP = (4096, 256, 26, 64)
        E, PROJ, MAXD, NFLAT = (128, 32, 512, 528)
        dense_t = jax.random.normal(ks[0], (B, D_DENSE), dtype=jnp.float32)
        sparse_t = jax.random.normal(ks[1], (B, N_SP, D_SP), dtype=jnp.float32)
        Wd = jax.random.normal(ks[2], (E, D_DENSE), dtype=jnp.float32) / np.sqrt(D_DENSE)
        Ws = jax.random.normal(ks[3], (E, D_SP), dtype=jnp.float32) / np.sqrt(D_SP)
        Wsi = jax.random.normal(ks[4], (PROJ, N_SP), dtype=jnp.float32) / np.sqrt(N_SP)
        Wl = jax.random.normal(ks[5], (MAXD, NFLAT), dtype=jnp.float32) / np.sqrt(NFLAT)
        gd = jnp.ones((E,), jnp.float32)
        bd = jnp.zeros((E,), jnp.float32)
        gs = jnp.ones((E,), jnp.float32)
        bs = jnp.zeros((E,), jnp.float32)
        gsi = jnp.ones((PROJ,), jnp.float32)
        bsi = jnp.zeros((PROJ,), jnp.float32)
        gl = jnp.ones((MAXD,), jnp.float32)
        bl = jnp.zeros((MAXD,), jnp.float32)
        return {'dense_t': dense_t, 'sparse_t': sparse_t, 'Wd': Wd, 'gd': gd, 'bd': bd, 'Ws': Ws, 'gs': gs, 'bs': bs, 'Wsi': Wsi, 'gsi': gsi, 'bsi': bsi, 'Wl': Wl, 'gl': gl, 'bl': bl, 'dims_in_use': 384}
    _L0_rec_all = _L0_rec_setup()
    _L0_rec_in = {k: v for k, v in _L0_rec_all.items() if k in ('Wd', 'gd', 'bd', 'Ws', 'gs', 'bs', 'Wsi', 'gsi', 'bsi', 'Wl', 'gl', 'bl')}
    del _L0_rec_all
    return {'r_dense_t': r_dense_t, 'ids': ids, 'tbl_0': tbl_0, 'tbl_1': tbl_1, 'tbl_2': tbl_2, 'tbl_3': tbl_3, 'tbl_4': tbl_4, 'tbl_5': tbl_5, 'tbl_6': tbl_6, 'tbl_7': tbl_7, 'tbl_8': tbl_8, 'tbl_9': tbl_9, 'tbl_10': tbl_10, 'tbl_11': tbl_11, 'tbl_12': tbl_12, 'tbl_13': tbl_13, 'tbl_14': tbl_14, 'tbl_15': tbl_15, 'tbl_16': tbl_16, 'tbl_17': tbl_17, 'tbl_18': tbl_18, 'tbl_19': tbl_19, 'tbl_20': tbl_20, 'tbl_21': tbl_21, 'tbl_22': tbl_22, 'tbl_23': tbl_23, 'tbl_24': tbl_24, 'tbl_25': tbl_25, 'W_top1': W_top1, 'b_top1': b_top1, 'W_top2': W_top2, 'b_top2': b_top2, 'W_top3': W_top3, 'L0_rec_Wd': _L0_rec_in['Wd'], 'L0_rec_gd': _L0_rec_in['gd'], 'L0_rec_bd': _L0_rec_in['bd'], 'L0_rec_Ws': _L0_rec_in['Ws'], 'L0_rec_gs': _L0_rec_in['gs'], 'L0_rec_bs': _L0_rec_in['bs'], 'L0_rec_Wsi': _L0_rec_in['Wsi'], 'L0_rec_gsi': _L0_rec_in['gsi'], 'L0_rec_bsi': _L0_rec_in['bsi'], 'L0_rec_Wl': _L0_rec_in['Wl'], 'L0_rec_gl': _L0_rec_in['gl'], 'L0_rec_bl': _L0_rec_in['bl']}

def reference(r_dense_t, ids, tbl_0, tbl_1, tbl_2, tbl_3, tbl_4, tbl_5, tbl_6, tbl_7, tbl_8, tbl_9, tbl_10, tbl_11, tbl_12, tbl_13, tbl_14, tbl_15, tbl_16, tbl_17, tbl_18, tbl_19, tbl_20, tbl_21, tbl_22, tbl_23, tbl_24, tbl_25, W_top1, b_top1, W_top2, b_top2, W_top3, L0_rec_Wd, L0_rec_gd, L0_rec_bd, L0_rec_Ws, L0_rec_gs, L0_rec_bs, L0_rec_Wsi, L0_rec_gsi, L0_rec_bsi, L0_rec_Wl, L0_rec_gl, L0_rec_bl):
    import jax
    import jax.numpy as jnp

    def _L0_rec_ref(dense_t, sparse_t, Wd, gd, bd, Ws, gs, bs, Wsi, gsi, bsi, Wl, gl, bl, dims_in_use):
        import jax, jax.numpy as jnp
        import numpy as np
        EPS = 1e-05
        NI = 33
        TRIL_I, TRIL_J = np.tril_indices(NI, k=-1)

        def layer_norm(x, g, b):
            m = jnp.mean(x, axis=-1, keepdims=True)
            v = jnp.mean(jnp.square(x - m), axis=-1, keepdims=True)
            return (x - m) * jax.lax.rsqrt(v + EPS) * g + b
        x = layer_norm(dense_t @ Wd.T, gd, bd)
        y = layer_norm(jnp.einsum('bnd,ed->bne', sparse_t, Ws), gs, bs)
        y = jnp.einsum('bne,pn->bep', y, Wsi)
        y = layer_norm(y, gsi, bsi)
        y = jnp.swapaxes(y, 1, 2)
        T = jnp.concatenate([x[:, None, :], y], axis=1)
        Z = jnp.einsum('bnd,bmd->bnm', T, T)
        Zflat = Z[:, TRIL_I, TRIL_J]
        out = layer_norm(Zflat @ Wl.T, gl, bl)
        maxd = out.shape[-1]
        mask = (jnp.arange(maxd) < dims_in_use).astype(out.dtype)
        return out * mask
    e = jnp.stack([tbl_0[ids[:, 0]], tbl_1[ids[:, 1]], tbl_2[ids[:, 2]], tbl_3[ids[:, 3]], tbl_4[ids[:, 4]], tbl_5[ids[:, 5]], tbl_6[ids[:, 6]], tbl_7[ids[:, 7]], tbl_8[ids[:, 8]], tbl_9[ids[:, 9]], tbl_10[ids[:, 10]], tbl_11[ids[:, 11]], tbl_12[ids[:, 12]], tbl_13[ids[:, 13]], tbl_14[ids[:, 14]], tbl_15[ids[:, 15]], tbl_16[ids[:, 16]], tbl_17[ids[:, 17]], tbl_18[ids[:, 18]], tbl_19[ids[:, 19]], tbl_20[ids[:, 20]], tbl_21[ids[:, 21]], tbl_22[ids[:, 22]], tbl_23[ids[:, 23]], tbl_24[ids[:, 24]], tbl_25[ids[:, 25]]], axis=1)
    z = _L0_rec_ref(r_dense_t, e, L0_rec_Wd, L0_rec_gd, L0_rec_bd, L0_rec_Ws, L0_rec_gs, L0_rec_bs, L0_rec_Wsi, L0_rec_gsi, L0_rec_bsi, L0_rec_Wl, L0_rec_gl, L0_rec_bl, 384)
    z = z.reshape(z.shape[0], -1)
    h = jnp.concatenate([z, r_dense_t], axis=1)
    h = jnp.maximum(h @ W_top1 + b_top1, 0.0)
    h = jnp.maximum(h @ W_top2 + b_top2, 0.0)
    y = h @ W_top3
    return y

_drawn_inputs = setup_inputs


def setup_inputs(seed=0):
    import zlib

    import numpy as np

    out = dict(_drawn_inputs(seed))
    spreads = {'b_top1': (0.0, 0.1),
     'b_top2': (0.0, 0.1),
     'L0_rec_gd': (1.0, 0.6),
     'L0_rec_bd': (0.0, 0.8),
     'L0_rec_gs': (1.0, 0.6),
     'L0_rec_bs': (0.0, 0.1),
     'L0_rec_gsi': (1.0, 0.2),
     'L0_rec_bsi': (0.0, 0.1),
     'L0_rec_gl': (1.0, 0.2),
     'L0_rec_bl': (0.0, 0.1)}
    factors = {}
    for name, (base, spread) in spreads.items():
        noise = np.random.default_rng([zlib.crc32(name.encode()), seed]).standard_normal(out[name].shape)
        drawn = base * np.exp(spread * noise) if base else spread * noise
        out[name] = jnp.asarray(drawn.astype(out[name].dtype))
    for name, factor in factors.items():
        out[name] = (out[name] * factor).astype(out[name].dtype)
    return out
```

```python
from contextlib import ExitStack

import numpy as np

import concourse.bass as bass
from concourse import mybir

F32 = mybir.dt.float32
I32 = mybir.dt.int32
ALU = mybir.AluOpType
ACT = mybir.ActivationFunctionType
AX = mybir.AxisListType.X

EPS = 1e-5
VOCAB = [1000, 1000, 1000, 125000, 12500, 12500, 12500, 1000, 12500, 12500, 1000, 125000, 125000,
         12500, 12500, 1000, 1250, 12500, 1000, 1000, 1250, 1000, 1000, 1250, 1000, 1250]
B = 2048
NF = len(VOCAB)
D = 64
E = 128
NP = 32
DD = 256
ML = 512
USED = 384
H1, H2 = 512, 256

SQ = 4
ROWS = SQ * NF
GU = 8
SU = SQ * GU
UB = 4
SB = UB * SU
GB = UB * GU
NB = B // SB
NG = B // SQ
SLOTS = NP + 2
KC = 5
NK = 18
ZROW = NP * SLOTS
PACK = GU * SLOTS
ZPAD = 3 + NP * (SLOTS + 1)

COL_SUM, COL_ONE, COL_ONES = 31, 63, 64


def pair_at(p, k):
    row, slot = divmod(p * SLOTS + 2 + p + k, SLOTS)
    if row >= NP or slot < 2 or slot - 2 == row:
        return None
    return max(row, slot - 2), min(row, slot - 2)


def interaction_rows():
    at = [pair_at(p, k + 1) for k in range(NK) for p in range(NP)]
    taken, rows = set(), []
    for pair in at:
        if pair is None or pair in taken:
            rows.append((-1, NP + 1, NP + 1))
            continue
        taken.add(pair)
        i, j = pair[0] + 1, pair[1] + 1
        rows.append((i * (i - 1) // 2 + j, pair[0], pair[1]))
    rows += [(-1, NP + 1, NP + 1)] * NP
    rows += [((p + 1) * p // 2, p, NP) for p in range(NP)]
    assert len(taken) == NP * (NP - 1) // 2 and len(rows) == KC * 128
    return rows


def dlrm_kernel(nc, a):
    scratch = nc.dram_tensor("products", (NB, 128, GB, SLOTS), F32, kind="Internal").ap()
    with ExitStack() as ctx:
        def sb(name, shape, dt=F32):
            return ctx.enter_context(nc.sbuf_tensor(name, shape, dt))

        def pb(name):
            return ctx.enter_context(nc.psum_tensor(name, [128, 512], F32))

        def sem(name):
            return ctx.enter_context(nc.semaphore(name))

        eye = sb("eye", [128, 128])
        centre = sb("centre", [128, 128])
        masks = sb("masks", [128, 3, KC, 128])
        row_base = sb("row_base", [ROWS, 1])
        last_one = sb("last_one", [ROWS, D + 1])
        ws = sb("ws", [E, D])
        gs_bs = sb("gs_bs", [E, 2])
        wc = sb("wc", [E, D])
        wc_gs = sb("wc_gs", [E, D + 1])
        wy = sb("wy", [D + 1, E])
        gram = sb("gram", [128, 128])
        wsi = sb("wsi", [ROWS, SQ, NP])
        wsi_sum = sb("wsi_sum", [ROWS, SQ])
        wsi_c = sb("wsi_c", [ROWS, SQ, NP])
        wd = sb("wd", [128, 2, E])
        gd_b = sb("gd_b", [128, E])
        bd_b = sb("bd_b", [128, E])
        w1z = sb("w1z", [128, 3, H1])
        w1 = sb("w1", [128, 5, H1])
        gl_bl = sb("gl_bl", [128, 2, 3])
        b1 = sb("b1", [128, 4])
        b1z = sb("b1z", [128, 4])
        w2 = sb("w2", [128, 4, H2])
        b2 = sb("b2", [128, 2])
        w3 = sb("w3", [128, 2])
        wl = sb("wl", [128, KC, ML])
        wk = sb("wk", [128, KC, ML])
        pair_gb = sb("pair_gb", [128, 4, KC])
        pair_x = sb("pair_x", [128, 4, KC])
        fold = sb("fold", [128, KC, 128])
        ids = sb("ids", [128, 4, ROWS], I32)
        ids_f = sb("ids_f", [128, 4, ROWS])
        index = sb("index", [ROWS, NG + UB * GU], I32)
        index_now = sb("index_now", [ROWS, UB, GU], I32)
        rows = sb("rows", [ROWS, UB, GU, D])
        et = sb("et", [128, GU // 2, ROWS])
        prod = sb("prod", [ROWS, GU, D])
        var_e = sb("var_e", [ROWS, GU])
        var_g = sb("var_g", [ROWS, GU])
        sd_e = sb("sd_e", [ROWS, GU])
        rs_e = sb("rs_e", [ROWS, GU])
        rows_n = sb("rows_n", [ROWS, GU, D])
        ut = sb("ut", [D + 1, GU, SQ * NP])
        y_sq = sb("y_sq", [E, SU, NP])
        y_sum = sb("y_sum", [E, SU])
        y_sd = sb("y_sd", [E, SU])
        y_rs = sb("y_rs", [E, SU])
        feat = sb("feat", [E, UB, SU, SLOTS])
        zs = sb("zs", [128, 2, GU, SLOTS])
        dense_x = sb("dense_x", [128, DD])
        dense_m = sb("dense_m", [128, DD])
        dt = sb("dt", [128, 4, 128])
        x_stat = sb("x_stat", [128, 6])
        x_mv = sb("x_mv", [128, 2])
        x_sd = sb("x_sd", [128, 1])
        x_rs = sb("x_rs", [128, 1])
        x_hat = sb("x_hat", [128, E])
        x_g = sb("x_g", [128, E])
        x_full = sb("x_full", [128, E])
        x_sum = sb("x_sum", [128, 1])
        zb = sb("zb", [128, ZPAD])
        zt = sb("zt", [128, KC, 128])
        l_stat = sb("l_stat", [128, 6])
        l_mv = sb("l_mv", [128, 2])
        l_sd = sb("l_sd", [128, 1])
        l_rs = sb("l_rs", [128, 1])
        z_hat = sb("z_hat", [128, USED])
        hz = sb("hz", [128, 3, 128])
        h1 = sb("h1", [128, 4, 128])
        h2 = sb("h2", [128, 2, 128])
        y_row = sb("y_row", [1, NB, GB, SQ])
        eps_col = sb("eps_col", [128, 1])

        p_t, p_q, p_u, p_z, p_a, p_b = (pb(n) for n in ("p_t", "p_q", "p_u", "p_z", "p_a", "p_b"))
        p_y = ctx.enter_context(nc.psum_tensor("p_y", [128, 1024], F32))

        skew = zb[:, 3:3 + NP * (SLOTS + 1)].rearrange("b (p k) -> b p k", k=SLOTS + 1)
        plain = zb[:, 0:ZROW].rearrange("b (p c) -> b p c", c=SLOTS)

        s_ids = sem("s_ids")
        s_eye = sem("s_eye")
        s_first = sem("s_first")
        s_rest = sem("s_rest")
        s_set = sem("s_set")
        s_pe0 = sem("s_pe0")
        s_dve0 = sem("s_dve0")
        gathered = [sem(f"gathered{j}") for j in range(UB)]
        index_ready = sem("index_ready")
        et_put = sem("et_put")
        et_ready = sem("et_ready")
        q_done = sem("q_done")
        q_used = sem("q_used")
        var_summed = sem("var_summed")
        var_ready = sem("var_ready")
        sd_ready = sem("sd_ready")
        rs_ready = sem("rs_ready")
        rows_ready = sem("rows_ready")
        u_done = sem("u_done")
        ut_ready = sem("ut_ready")
        y_done = sem("y_done")
        sq_ready = sem("sq_ready")
        y_summed = sem("y_summed")
        y_sd_ready = sem("y_sd_ready")
        y_rs_ready = sem("y_rs_ready")
        y_ready = sem("y_ready")
        z_done = sem("z_done")
        zs_ready = sem("zs_ready")
        z_stored = [sem(f"z_stored{m}") for m in range(2)]
        dense_x_in = sem("dense_x_in")
        dense_m_in = sem("dense_m_in")
        dt_put = sem("dt_put")
        dt_ready = sem("dt_ready")
        x_done = sem("x_done")
        x_chain = sem("x_chain")
        x_var_ready = sem("x_var_ready")
        x_sd_ready = sem("x_sd_ready")
        x_ready = sem("x_ready")
        xt_done = sem("xt_done")
        xt_ready = sem("xt_ready")
        zb_in = sem("zb_in")
        read_begun = sem("read_begun")
        gather_begun = sem("gather_begun")
        sum_put = sem("sum_put")
        zt_done = sem("zt_done")
        zt_ready = sem("zt_ready")
        pack_done = sem("pack_done")
        pack_ready = sem("pack_ready")
        l_done = sem("l_done")
        l_chain = sem("l_chain")
        l_var_ready = sem("l_var_ready")
        l_sd_ready = sem("l_sd_ready")
        z_hat_ready = sem("z_hat_ready")
        hz_done = sem("hz_done")
        hz_ready = sem("hz_ready")
        h1_done = sem("h1_done")
        h1_ready = sem("h1_ready")
        h2_done = sem("h2_done")
        h2_ready = sem("h2_ready")
        out_done = sem("out_done")
        out_ready = sem("out_ready")
        s_out = sem("s_out")
        l_rs_ready = sem("l_rs_ready")
        l_stat_ready = sem("l_stat_ready")
        x_sum_ready = sem("x_sum_ready")

        def after(eng, semaphore, count):
            if not isinstance(count, int) or count > 0:
                eng.wait_ge(semaphore, count)

        def stages(i, n):
            return n < NB, 1 <= n <= NB, 2 <= n

        def iterations(eng, body):
            body(0, 0)
            body(1, 1)
            with eng.Fori(2, NB) as i:
                body(i, 2)
            body(NB, NB)
            body(NB + 1, NB + 1)

        N_FIRST, N_REST = 5, 13
        block = ctx.enter_context(nc.Block())

        @block.sync
        def _(sp):
            sp.dma_start(ids[:], a["ids"].rearrange("(t g s) f -> g t (s f)", g=128, s=SQ)).then_inc(s_ids, 16)
            sp.dma_start(eye[:], a["eye"]).then_inc(s_eye, 16)
            sp.dma_start(row_base[:], a["row_base"]).then_inc(s_eye, 16)
            sp.dma_start(ws[:], a["Ws"]).then_inc(s_first, 16)
            sp.dma_start(centre[:], a["centre"]).then_inc(s_first, 16)
            sp.dma_start(gs_bs[:], a["gs_bs"]).then_inc(s_first, 16)
            sp.dma_start(wsi[:], a["Wsi_blocks"]).then_inc(s_first, 16)
            sp.dma_start(last_one[:], a["last_one"]).then_inc(s_first, 16)
            sp.dma_start(wd[:], a["WdT"].rearrange("(c p) e -> p c e", p=128)).then_inc(s_rest, 16)
            sp.dma_start(gd_b[:], a["gd_rows"]).then_inc(s_rest, 16)
            sp.dma_start(bd_b[:], a["bd_rows"]).then_inc(s_rest, 16)
            sp.dma_start(wl[:], a["Wl_rows"].rearrange("(c p) m -> p c m", p=128)).then_inc(s_rest, 16)
            sp.dma_start(pair_gb[:], a["pair_gb"]).then_inc(s_rest, 16)
            sp.dma_start(masks[:], a["masks"]).then_inc(s_rest, 16)
            sp.dma_start(w1z[:], a["W1"][0:USED, :].rearrange("(c p) m -> p c m", p=128)).then_inc(s_rest, 16)
            sp.dma_start(w1[:, 3:5, :], a["W1"][ML:ML + DD, :].rearrange("(c p) m -> p c m", p=128)).then_inc(s_rest, 16)
            sp.dma_start(gl_bl[:], a["gl_bl"]).then_inc(s_rest, 16)
            sp.dma_start(b1[:], a["b1"]).then_inc(s_rest, 16)
            sp.dma_start(w2[:], a["W2"].rearrange("(c p) m -> p c m", p=128)).then_inc(s_rest, 16)
            sp.dma_start(b2[:], a["b2"]).then_inc(s_rest, 16)
            sp.dma_start(w3[:], a["W3"]).then_inc(s_rest, 16)

            dense = a["dense"].rearrange("(n g s) d -> n s g d", g=GB, s=SQ)

            def body(i, n):
                units, layer, top = stages(i, n)
                if units:
                    after(sp, dt_put, i)
                    for s in range(SQ):
                        sp.dma_start(dense_x[32 * s:32 * s + 32, :], dense[i, s]).then_inc(dense_x_in, 16)
                if top:
                    after(sp, dt_put, i)
                    for s in range(SQ):
                        sp.dma_start(dense_m[32 * s:32 * s + 32, :], dense[i - 2, s]).then_inc(dense_m_in, 16)
                for j in range(UB):
                    if (j < 3 and layer) or (j == 3 and units):
                        unit, block_of, quarter = UB * i + j - 3, (i - 1 if j < 3 else i), (j - 3) % UB
                        sp.wait_ge(zs_ready, unit + 1)
                        sp.dma_start(scratch[block_of, :, GU * quarter:GU * quarter + GU, :],
                                     zs[:, (j + 1) % 2]).then_inc(z_stored[(j + 1) % 2], 16)
                    if j == 2 and layer:
                        for m in range(2):
                            sp.wait_ge(z_stored[m], 32 * i)
                        sp.sem_inc(read_begun, 1)
                        for s in range(SQ):
                            sp.dma_start(plain[32 * s:32 * s + 32],
                                         scratch[i - 1, 32 * s:32 * s + 32, :, :].rearrange("p g c -> g p c")
                                         ).then_inc(zb_in, 16)

            sp.wait_ge(s_set, 1)
            iterations(sp, body)
            sp.wait_ge(out_ready, NB)
            sp.dma_start(a["out"].rearrange("(a b) c -> a (b c)", a=1), y_row[:].rearrange("p n g s -> p (n g s)")).then_inc(s_out, 16)
            sp.wait_ge(s_out, 16)

        @block.gpsimd
        def _(pool):
            def body(i, n):
                for j in range(UB):
                    pool.wait_ge(index_ready, UB * i + j + 1)
                    pool.sem_inc(gather_begun, 1)
                    for g in range(GU):
                        pool.indirect_dma_start(
                            out=rows[:, j, g, :], out_offset=None, in_=a["table"],
                            in_offset=bass.IndirectOffsetOnAxis(ap=index_now[:, j, g:g + 1], axis=0),
                        ).then_inc(gathered[j], 16)
            body(0, 0)
            with pool.Fori(1, NB) as i:
                body(i, 1)

        @block.tensor
        def _(pe):
            pe.wait_ge(s_eye, 32)
            pe.wait_ge(s_dve0, 1)
            for t in range(4):
                last = nc.tensor.transpose(p_a[0:ROWS, 128 * t:128 * t + 128], ids_f[:, t, :], eye[:])
            last.then_inc(s_pe0, 1)
            pe.wait_ge(s_first, 16 * N_FIRST)
            nc.tensor.matmul(p_b[:, 0:D], centre[:], ws[:], start=True, stop=True).then_inc(s_pe0, 1)
            pe.wait_ge(s_dve0, 3)
            nc.tensor.transpose(p_t[0:D + 1, 0:E], wc_gs[:], eye[:])
            nc.tensor.matmul(p_q[0:D, 0:D], wc[:], wc[:], start=True, stop=True)
            nc.tensor.matmul(p_q[D:2 * D, 0:D], wc[:], wc[:], start=True, stop=True).then_inc(s_pe0, 1)
            pe.wait_ge(s_dve0, 4)
            nc.tensor.matmul(p_u[0:D + 1, 0:SQ * NP], last_one[:], wsi_c[:].rearrange("r s p -> r (s p)"),
                             start=True, stop=True).then_inc(s_pe0, 1)
            pe.wait_ge(s_rest, 16 * N_REST)
            for m in range(4):
                for c in range(3):
                    last = nc.tensor.matmul(p_b[:, 128 + m:129 + m], w1z[:, c, 128 * m:128 * m + 128],
                                            gl_bl[:, 1, c:c + 1], start=c == 0, stop=c == 2)
            last.then_inc(s_pe0, 1)
            pe.wait_ge(s_dve0, 6)
            for c in range(KC):
                last = nc.tensor.matmul(p_a[:], fold[:, c, :], wl[:, c, :], start=c == 0, stop=c == KC - 1)
            last.then_inc(s_pe0, 1)
            pe.wait_ge(s_dve0, 7)

            def body(i, n):
                units, layer, top = stages(i, n)
                for j in range(UB):
                    k = UB * i + j
                    now, lag1, lag3 = units, (layer if j == 0 else units), (layer if j < 3 else units)
                    if now:
                        pe.wait_ge(gathered[j], 16 * GU * (i + 1))
                        after(pe, et_ready, k)
                        for m in range(GU // 2):
                            last = nc.tensor.transpose(
                                p_t[:, ROWS * m:ROWS * m + ROWS],
                                rows[:, j, 2 * m:2 * m + 2, :].rearrange("r g d -> r (g d)"), eye[0:ROWS, 0:ROWS])
                        last.then_inc(et_put, 1)
                    if lag3:
                        jj = (j - 3) % UB
                        pe.wait_ge(y_ready, k - 2)
                        pe.wait_ge(xt_ready, i if j < 3 else i + 1)
                        after(pe, zs_ready, k - 3)
                        if j == 0:
                            after(pe, pack_ready, i - 1)
                        for g in range(GU):
                            for s in range(SQ):
                                f = feat[:, jj, SQ * g + s, :]
                                last = nc.tensor.matmul(p_z[32 * s:32 * s + 32, SLOTS * g:SLOTS * g + SLOTS],
                                                        f[:, 2:SLOTS], f, start=True, stop=True)
                        last.then_inc(z_done, 1)
                    if j == 1 and (units or top):
                        after(pe, zt_ready, i - 1)
                        if units:
                            pe.wait_ge(dense_x_in, 64 * (i + 1))
                            for c in range(2):
                                last = nc.tensor.transpose(p_a[:, 128 * c:128 * c + 128],
                                                           dense_x[:, 128 * c:128 * c + 128], eye[:])
                        if top:
                            pe.wait_ge(dense_m_in, 64 * (i - 1))
                            for c in range(2):
                                last = nc.tensor.transpose(p_a[:, 256 + 128 * c:384 + 128 * c],
                                                           dense_m[:, 128 * c:128 * c + 128], eye[:])
                        last.then_inc(dt_put, 1)
                    if lag1:
                        pe.wait_ge(rows_ready, k)
                        after(pe, ut_ready, 2 * (k - 1))
                        for g in range(GU):
                            h = g % 2
                            last = nc.tensor.matmul(p_u[D * h:D * h + D, 128 * (g // 2):128 * (g // 2) + 128],
                                                    rows_n[:, g, :], wsi_c[:].rearrange("r s p -> r (s p)"),
                                                    start=True, stop=True)
                        last.then_inc(u_done, 1)
                    if now:
                        pe.wait_ge(et_ready, k + 1)
                        after(pe, q_used, k)
                        for m in range(GU // 2):
                            last = nc.tensor.matmul(p_q[0:ROWS, 128 * m:128 * m + 128], et[:, m, :], gram[:],
                                                    start=True, stop=True)
                        last.then_inc(q_done, 1)
                    if j == 2 and units:
                        pe.wait_ge(x_ready, i + 1)
                        nc.tensor.transpose(p_a[:, 128:256], x_full[:], eye[:]).then_inc(xt_done, 1)
                    if j == 2 and top:
                        pe.wait_ge(z_hat_ready, i - 1)
                        for c in range(3):
                            last = nc.tensor.transpose(p_b[:, 128 * c:128 * c + 128],
                                                       z_hat[:, 128 * c:128 * c + 128], eye[:])
                        last.then_inc(hz_done, 1)
                    if lag1:
                        pe.wait_ge(ut_ready, 2 * k)
                        after(pe, y_ready, k - 1)
                        for h in range(2):
                            last = nc.tensor.matmul(p_y[:, 512 * h:512 * h + 512], wy[:],
                                                    ut[:, 4 * h:4 * h + 4, :].rearrange("d g c -> d (g c)"),
                                                    start=True, stop=True)
                        last.then_inc(y_done, 1)
                    if j == 0 and top:
                        pe.wait_ge(zt_ready, i - 1)
                        pe.wait_ge(pack_ready, i - 1)
                        after(pe, out_ready, i - 2)
                        for c in range(3):
                            nc.tensor.matmul(p_b[:], zt[:, c, :], wk[:, c, :], start=c == 0, stop=False)
                    if j == 1:
                        if top:
                            for c in (3, 4):
                                last = nc.tensor.matmul(p_b[:], zt[:, c, :], wk[:, c, :], start=False, stop=c == 4)
                            last.then_inc(l_done, 1)
                        if units:
                            pe.wait_ge(dt_ready, i + 1)
                            for c in range(2):
                                last = nc.tensor.matmul(p_a[:, 0:E], dt[:, c, :], wd[:, c, :],
                                                        start=c == 0, stop=c == 1)
                            last.then_inc(x_done, 1)
                    if j == 2 and top:
                        pe.wait_ge(dt_ready, i + 1)
                        pe.wait_ge(hz_ready, i - 1)
                        for m in range(4):
                            for c in range(5):
                                last = nc.tensor.matmul(p_b[:, 128 * m:128 * m + 128],
                                                        w1[:, c, 128 * m:128 * m + 128],
                                                        hz[:, c, :] if c < 3 else dt[:, c - 1, :],
                                                        start=c == 0, stop=c == 4)
                        last.then_inc(h1_done, 1)
                    if j == 3 and top:
                        pe.wait_ge(h1_ready, 4 * (i - 1))
                        for m in range(2):
                            for c in range(4):
                                last = nc.tensor.matmul(p_b[:, 128 * m:128 * m + 128],
                                                        w2[:, c, 128 * m:128 * m + 128], h1[:, c, :],
                                                        start=c == 0, stop=c == 3)
                        last.then_inc(h2_done, 1)
                    if j == 3 and layer:
                        pe.wait_ge(zb_in, 64 * i)
                        if units:
                            pe.wait_ge(xt_ready, i + 1)
                        for k4 in range(16):
                            q = k4 % 4
                            last = nc.tensor.matmul(p_a[32 * q:32 * q + 32, 32 * (k4 - q):32 * (k4 - q) + 128],
                                                    skew[:, :, k4], eye[:], start=True, stop=True)
                        last.then_inc(zt_done, 1)
                        pe.wait_ge(sum_put, i)
                        pe.wait_ge(zs_ready, UB * i + 1 if units else UB * i)
                        for q, products in enumerate((skew[:, :, 16], skew[:, :, 17], plain[:, :, 1], plain[:, :, 0])):
                            last = nc.tensor.matmul(p_z[32 * q:32 * q + 32, PACK:PACK + 128], products, eye[:],
                                                    start=True, stop=True)
                        last.then_inc(pack_done, 1)
                    if j == 3 and top:
                        pe.wait_ge(h2_ready, 2 * (i - 1))
                        for c in range(2):
                            last = nc.tensor.matmul(p_b[0:1, 256:384], w3[:, c:c + 1], h2[:, c, :],
                                                    start=c == 0, stop=c == 1)
                        last.then_inc(out_done, 1)

            iterations(pe, body)

        @block.scalar
        def _(act):
            act.wait_ge(s_set, 1)

            def body(i, n):
                units, layer, top = stages(i, n)
                for j in range(UB):
                    k = UB * i + j
                    now, lag1, lag3 = units, (layer if j == 0 else units), (layer if j < 3 else units)
                    if now:
                        act.wait_ge(et_put, k + 1)
                        after(act, q_done, k)
                        nc.scalar.copy(et[:].rearrange("d m r -> d (m r)"), p_t[:, 0:ROWS * GU // 2]).then_inc(et_ready, 1)
                    if j == 2 and units:
                        act.wait_ge(x_var_ready, i + 1)
                        nc.scalar.activation(x_sd[:], x_mv[:, 1:2], ACT.Sqrt, bias=eps_col[:]).then_inc(x_sd_ready, 1)
                    if j == 2 and top:
                        act.wait_ge(l_var_ready, i - 1)
                        nc.scalar.activation(l_sd[:], l_mv[:, 1:2], ACT.Sqrt, bias=eps_col[:]).then_inc(l_sd_ready, 1)
                    if lag3:
                        act.wait_ge(z_done, k - 2)
                        after(act, z_stored[(j + 1) % 2], 16 * (2 * i + (j - 3) // 2))
                        nc.scalar.copy(zs[:, (j + 1) % 2].rearrange("r g c -> r (g c)"), p_z[:, 0:GU * SLOTS]).then_inc(zs_ready, 1)
                    if j == 1 and (units or top):
                        lo, hi = (0 if units else 2), (4 if top else 2)
                        act.wait_ge(dt_put, i + 1)
                        after(act, x_done, i if units else NB)
                        after(act, h1_done, i - 2)
                        nc.scalar.copy(dt[:, lo:hi, :].rearrange("d c b -> d (c b)"),
                                       p_a[:, 128 * lo:128 * hi]).then_inc(dt_ready, 1)
                    if lag1:
                        act.wait_ge(u_done, k)
                        after(act, y_done, k - 1)
                        for h in range(2):
                            nc.scalar.copy(ut[0:D, :, :].rearrange("d (g h) c -> d h g c", h=2)[:, h],
                                           p_u[D * h:D * h + D, :].rearrange("d (g c) -> d g c", g=GU // 2)
                                           ).then_inc(ut_ready, 1)
                    if j == 2 and units:
                        act.wait_ge(xt_done, i + 1)
                        after(act, z_done, UB * i)
                        nc.scalar.copy(feat[:].rearrange("e u (g s) c -> e c s (u g)", s=SQ)[:, 0],
                                       p_a[:, 128:256].rearrange("e (s g) -> e s g", s=SQ)).then_inc(xt_ready, 1)
                    if now:
                        act.wait_ge(var_ready, k + 1)
                        nc.scalar.activation(sd_e[:], var_g[:], ACT.Sqrt).then_inc(sd_ready, 1)
                    if lag1:
                        act.wait_ge(y_done, k)
                        after(act, y_summed, k - 1)
                        nc.scalar.activation(y_sq[:].rearrange("e b p -> e (b p)"), p_y[:], ACT.Square).then_inc(sq_ready, 1)
                        act.wait_ge(y_summed, k)
                        nc.scalar.activation(y_sd[:], y_sum[:], ACT.Sqrt, bias=eps_col[:], scale=1.0 / NP).then_inc(y_sd_ready, 1)
                    if j == 2 and top:
                        act.wait_ge(h1_done, i - 1)
                        after(act, h2_done, i - 2)
                        for m in range(4):
                            nc.scalar.activation(h1[:, m, :], p_b[:, 128 * m:128 * m + 128], ACT.Relu,
                                                 bias=b1z[:, m:m + 1]).then_inc(h1_ready, 1)
                    if j == 3 and top:
                        act.wait_ge(h2_done, i - 1)
                        after(act, out_done, i - 2)
                        for m in range(2):
                            nc.scalar.activation(h2[:, m, :], p_b[:, 128 * m:128 * m + 128], ACT.Relu,
                                                 bias=b2[:, m:m + 1]).then_inc(h2_ready, 1)
                    if j == 3 and layer:
                        act.wait_ge(zt_done, i)
                        after(act, l_done, i - 1)
                        nc.scalar.copy(zt[:, 0:4, :].rearrange("r c b -> r (c b)"), p_a[:]).then_inc(zt_ready, 1)
                    if j == 3 and top:
                        act.wait_ge(out_done, i - 1)
                        nc.scalar.copy(y_row[:, i - 2, :, :].rearrange("p g s -> p s g"),
                                       p_b[0:1, 256:384].rearrange("p (s g) -> p s g", s=SQ)).then_inc(out_ready, 1)

            iterations(act, body)

        @block.vector
        def _(dve):
            dve.wait_ge(s_ids, 16)
            nc.vector.tensor_copy(ids_f[:], ids[:]).then_inc(s_dve0, 1)
            nc.vector.memset(index[:, NG:], 0).then_inc(l_chain, 1)
            nc.vector.memset(eps_col[:], EPS).then_inc(l_chain, 1)
            nc.vector.memset(feat[:, :, :, 1], 1.0).then_inc(l_chain, 1)
            nc.vector.memset(zb[:], 0.0).then_inc(l_chain, 1)
            nc.vector.memset(gram[:], 0.0).then_inc(l_chain, 1)
            dve.wait_ge(s_pe0, 1)
            nc.vector.tensor_scalar(index[:, 0:NG], p_a[0:ROWS, :], row_base[:], None, ALU.add).then_inc(l_chain, 1)
            dve.wait_ge(l_chain, 6)
            for j in range(UB):
                nc.vector.tensor_copy(index_now[:, j, :], index[:, GU * j:GU * j + GU]).then_inc(index_ready, 1)
            dve.wait_ge(s_pe0, 2)
            nc.vector.tensor_copy(wc[:], p_b[:, 0:D]).then_inc(s_dve0, 1)
            nc.vector.tensor_copy(wc_gs[:, D:D + 1], gs_bs[:, 1:2]).then_inc(l_chain, 1)
            dve.wait_ge(l_chain, 7)
            nc.vector.tensor_scalar(wc_gs[:, 0:D], p_b[:, 0:D], gs_bs[:, 0:1], None, ALU.mult).then_inc(s_dve0, 1)
            nc.vector.tensor_reduce(wsi_sum[:], wsi[:], AX, ALU.add).then_inc(l_chain, 1)
            dve.wait_ge(l_chain, 8)
            nc.vector.scalar_tensor_tensor(out=wsi_c[:], in0=wsi_sum[:].unsqueeze(2).to_broadcast([ROWS, SQ, NP]),
                                           scalar=-1.0 / NP, in1=wsi[:], op0=ALU.mult, op1=ALU.add).then_inc(s_dve0, 1)
            dve.wait_ge(s_pe0, 3)
            nc.vector.tensor_copy(wy[:], p_t[0:D + 1, 0:E]).then_inc(l_chain, 1)
            for h in range(2):
                nc.vector.tensor_scalar(gram[D * h:D * h + D, D * h:D * h + D], p_q[D * h:D * h + D, 0:D], 1.0 / E,
                                        None, ALU.mult).then_inc(l_chain, 1)
            dve.wait_ge(s_pe0, 4)
            nc.vector.tensor_copy(ut[D:D + 1, :, :], p_u[D:D + 1, 0:SQ * NP].unsqueeze(1).to_broadcast([1, GU, SQ * NP])
                                  ).then_inc(l_chain, 1)
            dve.wait_ge(s_rest, 16 * N_REST)
            for c in range(3):
                nc.vector.tensor_scalar(w1[:, c, :], w1z[:, c, :], gl_bl[:, 0, c:c + 1], None, ALU.mult).then_inc(l_chain, 1)
            dve.wait_ge(s_pe0, 5)
            nc.vector.tensor_tensor(b1z[:], p_b[:, 128:132], b1[:], ALU.add).then_inc(s_dve0, 1)
            for n, (u, v) in enumerate(((0, 1), (0, 3), (1, 2), (2, 3))):
                nc.vector.tensor_tensor(pair_x[:, n, :], pair_gb[:, u, :], pair_gb[:, v, :], ALU.mult).then_inc(l_chain, 1)
            dve.wait_ge(l_chain, 19)
            for c in range(KC):
                nc.vector.tensor_scalar(fold[:, c, :], masks[:, 0, c, :], pair_x[:, 1, c:c + 1], None, ALU.mult).then_inc(l_chain, 1)
                nc.vector.tensor_scalar(wk[:, c, :], wl[:, c, :], pair_x[:, 0, c:c + 1], None, ALU.mult).then_inc(l_chain, 1)
            for n in (1, 2):
                for c in range(KC):
                    if c == 0:
                        dve.wait_ge(l_chain, 29 if n == 1 else 34)
                    nc.vector.scalar_tensor_tensor(out=fold[:, c, :], in0=masks[:, n, c, :], scalar=pair_x[:, n + 1, c:c + 1],
                                                   in1=fold[:, c, :], op0=ALU.mult, op1=ALU.add).then_inc(l_chain, 1)
            dve.wait_ge(l_chain, 39)
            nc.vector.sem_inc(s_dve0, 1)
            dve.wait_ge(s_pe0, 6)
            nc.vector.tensor_tensor(wk[:, KC - 1, :], wk[:, KC - 1, :], p_a[:], ALU.add).then_inc(l_chain, 1)
            nc.vector.memset(skew[:, NP - 1:NP, 17], 1.0).then_inc(l_chain, 1)
            dve.wait_ge(l_chain, 41)
            nc.vector.sem_inc(s_dve0, 1)
            nc.vector.sem_inc(s_set, 1)

            def body(i, n):
                units, layer, top = stages(i, n)
                for j in range(UB):
                    k = UB * i + j
                    now, lag1 = units, (layer if j == 0 else units)
                    if j == 0 and layer:
                        after(dve, pack_done, i - 1)
                        nc.vector.tensor_copy(skew[:, NP - 1:NP, 16], x_sum[:]).then_inc(sum_put, 1)
                    if j == 2 and units:
                        dve.wait_ge(x_done, i + 1)
                        nc.vector.bn_stats(x_stat[:], p_a[:, 0:E]).then_inc(x_chain, 1)
                        dve.wait_ge(s_rest, 16 * N_REST)
                        dve.wait_ge(x_chain, 4 * i + 1)
                        nc.vector.bn_aggr(x_mv[:], x_stat[:]).then_inc(x_var_ready, 1)
                    if j == 2 and top:
                        dve.wait_ge(l_done, i - 1)
                        nc.vector.bn_stats(l_stat[:], p_b[:]).then_inc(l_stat_ready, 1)
                        dve.wait_ge(s_rest, 16 * N_REST)
                        dve.wait_ge(l_stat_ready, i - 1)
                        nc.vector.bn_aggr(l_mv[:], l_stat[:]).then_inc(l_var_ready, 1)
                    if j == 2 and units:
                        dve.wait_ge(x_sd_ready, i + 1)
                        nc.vector.reciprocal(x_rs[:], x_sd[:]).then_inc(x_chain, 1)
                        dve.wait_ge(x_chain, 4 * i + 2)
                        nc.vector.tensor_scalar(x_hat[:], p_a[:, 0:E], x_mv[:, 0:1], x_rs[:], ALU.subtract, ALU.mult
                                                ).then_inc(x_chain, 1)
                        dve.wait_ge(x_chain, 4 * i + 3)
                        nc.vector.tensor_tensor(x_g[:], x_hat[:], gd_b[:], ALU.mult).then_inc(x_chain, 1)
                        dve.wait_ge(x_chain, 4 * i + 4)
                        nc.vector.tensor_tensor(x_full[:], x_g[:], bd_b[:], ALU.add).then_inc(x_ready, 1)
                    if j == 2 and top:
                        dve.wait_ge(l_sd_ready, i - 1)
                        nc.vector.reciprocal(l_rs[:], l_sd[:]).then_inc(l_rs_ready, 1)
                        dve.wait_ge(l_rs_ready, i - 1)
                        nc.vector.tensor_scalar(z_hat[:], p_b[:, 0:USED], l_mv[:, 0:1], l_rs[:], ALU.subtract, ALU.mult
                                                ).then_inc(z_hat_ready, 1)
                    if j == 2 and units:
                        dve.wait_ge(x_ready, i + 1)
                        nc.vector.tensor_reduce(x_sum[:], x_full[:], AX, ALU.add).then_inc(x_sum_ready, 1)
                    if now:
                        dve.wait_ge(q_done, k + 1)
                        nc.vector.tensor_tensor(prod[:].rearrange("r g d -> r (g d)"), p_q[0:ROWS, :],
                                                rows[:, j, :, :].rearrange("r g d -> r (g d)"), ALU.mult).then_inc(q_used, 1)
                        dve.wait_ge(q_used, k + 1)
                        nc.vector.tensor_reduce(var_e[:], prod[:], AX, ALU.add).then_inc(var_summed, 1)
                        dve.wait_ge(var_summed, k + 1)
                        nc.vector.tensor_scalar(var_g[:], var_e[:], 0.0, EPS, ALU.max, ALU.add).then_inc(var_ready, 1)
                    if j == 2 and top:
                        dve.wait_ge(hz_done, i - 1)
                        nc.vector.tensor_copy(hz[:].rearrange("d c b -> d (c b)"), p_b[:, 0:USED]).then_inc(hz_ready, 1)
                    if now:
                        dve.wait_ge(sd_ready, k + 1)
                        nc.vector.reciprocal(rs_e[:], sd_e[:]).then_inc(rs_ready, 1)
                        dve.wait_ge(rs_ready, k + 1)
                        after(dve, u_done, k)
                        nc.vector.tensor_tensor(rows_n[:], rows[:, j, :, :], rs_e[:].unsqueeze(2).to_broadcast([ROWS, GU, D]),
                                                ALU.mult).then_inc(rows_ready, 1)
                        nc.vector.tensor_copy(index_now[:, j, :], index[:, bass.ds(GU * (k + UB), GU)]).then_inc(index_ready, 1)
                    if lag1:
                        jj = (j - 1) % UB
                        dve.wait_ge(sq_ready, k)
                        nc.vector.tensor_reduce(y_sum[:], y_sq[:], AX, ALU.add).then_inc(y_summed, 1)
                        dve.wait_ge(y_sd_ready, k)
                        nc.vector.reciprocal(y_rs[:], y_sd[:]).then_inc(y_rs_ready, 1)
                        dve.wait_ge(y_rs_ready, k)
                        after(dve, z_done, k - UB)
                        nc.vector.tensor_tensor(feat[:, jj, :, 2:SLOTS], p_y[:].rearrange("e (b p) -> e b p", p=NP),
                                                y_rs[:].unsqueeze(2).to_broadcast([E, SU, NP]), ALU.mult).then_inc(y_ready, 1)
                    if j == 3 and layer:
                        dve.wait_ge(pack_done, i)
                        after(dve, l_done, i - 1)
                        nc.vector.tensor_copy(zt[:, KC - 1, :], p_z[:, PACK:PACK + 128]).then_inc(pack_ready, 1)

            iterations(dve, body)


_TABLES = [f"tbl_{f}" for f in range(NF)]


def kernel(**inputs):
    import concourse.bacc as _bacc
    from concourse.bass_utils import run_bass_kernel_spmd as _run

    x = {k: np.asarray(v) for k, v in inputs.items()}
    pairs = interaction_rows()
    wl_cols = np.concatenate([x["L0_rec_Wl"].T, np.zeros((1, ML), np.float32)])
    first = np.array([r[1] for r in pairs]).reshape(KC, 128).T
    second = np.array([r[2] for r in pairs]).reshape(KC, 128).T
    gsi = np.concatenate([x["L0_rec_gsi"], np.array([1.0, 0.0], np.float32)])
    bsi = np.concatenate([x["L0_rec_bsi"], np.array([0.0, 0.0], np.float32)])
    wsi_blocks = np.zeros((SQ, NF, SQ, NP), np.float32)
    for s in range(SQ):
        wsi_blocks[s, :, s, :] = x["L0_rec_Wsi"].T
    masks = np.zeros((3, KC * 128, 128), np.float32)
    for n, (col, p, q) in enumerate(pairs):
        if col < 0:
            continue
        if q < NP:
            masks[0, n, COL_ONES + p] = 1.0
            masks[1, n, COL_ONES + q] = 1.0
            masks[2, n, COL_ONE] = float(E)
        else:
            masks[1, n, COL_SUM] = 1.0
    last_one = np.zeros((ROWS, D + 1), np.float32)
    last_one[:, D] = 1.0
    base = np.concatenate([[0], np.cumsum(VOCAB)[:-1]]).astype(np.float32)

    def cols(v):
        return v.reshape(-1, 128).T

    arrays = {
        "ids": x["ids"],
        "table": np.concatenate([x[t] for t in _TABLES]),
        "dense": x["r_dense_t"],
        "Ws": x["L0_rec_Ws"],
        "gs_bs": np.stack([x["L0_rec_gs"], x["L0_rec_bs"]], 1),
        "Wsi_blocks": wsi_blocks.reshape(ROWS, SQ, NP),
        "WdT": x["L0_rec_Wd"].T,
        "gd_rows": np.broadcast_to(x["L0_rec_gd"], (128, E)),
        "bd_rows": np.broadcast_to(x["L0_rec_bd"], (128, E)),
        "Wl_rows": wl_cols[[r[0] for r in pairs]],
        "pair_gb": np.stack([gsi[first], gsi[second], bsi[first], bsi[second]], 1),
        "W1": x["W_top1"],
        "gl_bl": np.stack([cols(x["L0_rec_gl"][:USED]), cols(x["L0_rec_bl"][:USED])], 1),
        "b1": cols(x["b_top1"]),
        "W2": x["W_top2"],
        "b2": cols(x["b_top2"]),
        "W3": x["W_top3"].reshape(2, 128).T,
        "eye": np.eye(128, dtype=np.float32),
        "centre": (np.eye(E) - 1.0 / E).astype(np.float32),
        "masks": masks.reshape(3, KC, 128, 128).transpose(2, 0, 1, 3),
        "last_one": last_one,
        "row_base": np.tile(base, SQ).reshape(ROWS, 1),
    }
    arrays = {k: np.ascontiguousarray(v) for k, v in arrays.items()}
    nc = _bacc.Bacc("TRN2", target_bir_lowering=False, num_devices=1)
    a = {k: nc.dram_tensor(f"in_{k}", v.shape, mybir.dt.from_np(v.dtype), kind="ExternalInput").ap()
         for k, v in arrays.items()}
    a["out"] = nc.dram_tensor("out_y", (B, 1), F32, kind="ExternalOutput").ap()
    dlrm_kernel(nc, a)
    r = _run(nc, [{f"in_{k}": v for k, v in arrays.items()}], core_ids=[0])
    return r.results[0]["out_y"]
```

```python
from contextlib import ExitStack

import numpy as np

import concourse.bass as bass
from concourse import mybir

F32 = mybir.dt.float32
I32 = mybir.dt.int32
ALU = mybir.AluOpType
ACT = mybir.ActivationFunctionType
AX = mybir.AxisListType.X

EPS = 1e-5
VOCAB = [1000, 1000, 1000, 125000, 12500, 12500, 12500, 1000, 12500, 12500, 1000, 125000, 125000,
         12500, 12500, 1000, 1250, 12500, 1000, 1000, 1250, 1000, 1000, 1250, 1000, 1250]
B = 2048
NF = len(VOCAB)
D = 64
E = 128
NP = 32
DD = 256
ML = 512
USED = 384
H1, H2 = 512, 256

SQ = 4
ROWS = SQ * NF
GU = 8
SU = SQ * GU
UB = 4
SB = UB * SU
GB = UB * GU
NB = B // SB
NG = B // SQ
SLOTS = NP + 2
KC = 5
NK = 18
ZROW = NP * SLOTS
PACK = 384
ZPAD = 3 + NP * (SLOTS + 1)

COL_SUM, COL_ONE, COL_ONES = 31, 63, 64


def pair_at(p, k):
    row, slot = divmod(p * SLOTS + 2 + p + k, SLOTS)
    if row >= NP or slot < 2 or slot - 2 == row:
        return None
    return max(row, slot - 2), min(row, slot - 2)


def interaction_rows():
    at = [pair_at(p, k + 1) for k in range(NK) for p in range(NP)]
    taken, rows = set(), []
    for pair in at:
        if pair is None or pair in taken:
            rows.append((-1, NP + 1, NP + 1))
            continue
        taken.add(pair)
        i, j = pair[0] + 1, pair[1] + 1
        rows.append((i * (i - 1) // 2 + j, pair[0], pair[1]))
    rows += [(-1, NP + 1, NP + 1)] * NP
    rows += [((p + 1) * p // 2, p, NP) for p in range(NP)]
    assert len(taken) == NP * (NP - 1) // 2 and len(rows) == KC * 128
    return rows


def dlrm_kernel(nc, a):
    scratch = nc.dram_tensor("products", (NB, 128, GB, SLOTS), F32, kind="Internal").ap()
    with ExitStack() as ctx:
        def sb(name, shape, dt=F32):
            return ctx.enter_context(nc.sbuf_tensor(name, shape, dt))

        def pb(name):
            return ctx.enter_context(nc.psum_tensor(name, [128, 512], F32))

        def sem(name):
            return ctx.enter_context(nc.semaphore(name))

        eye = sb("eye", [128, 128])
        centre = sb("centre", [128, 128])
        masks = sb("masks", [128, 3, KC, 128])
        row_base = sb("row_base", [ROWS, 1])
        last_one = sb("last_one", [ROWS, D + 1])
        ws = sb("ws", [E, D])
        gs_bs = sb("gs_bs", [E, 2])
        wc = sb("wc", [E, D])
        wc_gs = sb("wc_gs", [E, D + 1])
        wy = sb("wy", [D + 1, E])
        gram = sb("gram", [128, 128])
        wsi = sb("wsi", [ROWS, SQ, NP])
        wsi_sum = sb("wsi_sum", [ROWS, SQ])
        wsi_c = sb("wsi_c", [ROWS, SQ, NP])
        wd = sb("wd", [128, 2, E])
        gd_b = sb("gd_b", [128, E])
        bd_b = sb("bd_b", [128, E])
        w1z = sb("w1z", [128, 3, H1])
        w1 = sb("w1", [128, 5, H1])
        gl_bl = sb("gl_bl", [128, 2, 3])
        b1 = sb("b1", [128, 4])
        b1z = sb("b1z", [128, 4])
        w2 = sb("w2", [128, 4, H2])
        b2 = sb("b2", [128, 2])
        w3 = sb("w3", [128, 2])
        wl = sb("wl", [128, KC, ML])
        wk = sb("wk", [128, KC, ML])
        pair_gb = sb("pair_gb", [128, 4, KC])
        pair_x = sb("pair_x", [128, 4, KC])
        fold = sb("fold", [128, KC, 128])
        ids = sb("ids", [128, 4, ROWS], I32)
        ids_f = sb("ids_f", [128, 4, ROWS])
        index = sb("index", [ROWS, NG + UB * GU], I32)
        index_now = sb("index_now", [ROWS, UB, GU], I32)
        rows = sb("rows", [ROWS, UB, GU, D])
        et = sb("et", [128, GU // 2, ROWS])
        prod = sb("prod", [ROWS, GU, D])
        var_e = sb("var_e", [ROWS, GU])
        var_g = sb("var_g", [ROWS, GU])
        sd_e = sb("sd_e", [ROWS, GU])
        rs_e = sb("rs_e", [ROWS, GU])
        rows_n = sb("rows_n", [ROWS, GU, D])
        ut = sb("ut", [D + 1, GU, SQ * NP])
        y_sq = sb("y_sq", [E, SU, NP])
        y_sum = sb("y_sum", [E, SU])
        y_sd = sb("y_sd", [E, SU])
        y_rs = sb("y_rs", [E, SU])
        feat = sb("feat", [E, UB, SU, SLOTS])
        zs = sb("zs", [128, 2, GU, SLOTS])
        dense_x = sb("dense_x", [128, DD])
        dense_m = sb("dense_m", [128, DD])
        dt = sb("dt", [128, 4, 128])
        x_stat = sb("x_stat", [128, 6])
        x_mv = sb("x_mv", [128, 2])
        x_sd = sb("x_sd", [128, 1])
        x_rs = sb("x_rs", [128, 1])
        x_hat = sb("x_hat", [128, E])
        x_g = sb("x_g", [128, E])
        x_full = sb("x_full", [128, E])
        zb = sb("zb", [128, ZPAD])
        zt = sb("zt", [128, KC, 128])
        l_stat = sb("l_stat", [128, 6])
        l_mv = sb("l_mv", [128, 2])
        l_sd = sb("l_sd", [128, 1])
        l_rs = sb("l_rs", [128, 1])
        z_hat = sb("z_hat", [128, USED])
        hz = sb("hz", [128, 3, 128])
        h1 = sb("h1", [128, 4, 128])
        h2 = sb("h2", [128, 2, 128])
        y_row = sb("y_row", [1, NB, GB, SQ])
        eps_col = sb("eps_col", [128, 1])

        p_t, p_q, p_u, p_z, p_a, p_b = (pb(n) for n in ("p_t", "p_q", "p_u", "p_z", "p_a", "p_b"))
        p_y = ctx.enter_context(nc.psum_tensor("p_y", [128, 1024], F32))

        skew = zb[:, 3:3 + NP * (SLOTS + 1)].rearrange("b (p k) -> b p k", k=SLOTS + 1)
        plain = zb[:, 0:ZROW].rearrange("b (p c) -> b p c", c=SLOTS)

        ids_in = sem("ids_in")
        eye_in = sem("eye_in")
        first_in = sem("first_in")
        x_weights_in = sem("x_weights_in")
        top_weights_in = sem("top_weights_in")
        ids_float = sem("ids_float")
        ids_turned = sem("ids_turned")
        wc_done = sem("wc_done")
        wc_ready = sem("wc_ready")
        wy_done = sem("wy_done")
        wsi_ready = sem("wsi_ready")
        u_const_done = sem("u_const_done")
        prepared = sem("prepared")
        units_ready = sem("units_ready")
        bl_done = sem("bl_done")
        fold_ready = sem("fold_ready")
        fold_done = sem("fold_done")
        top_ready = sem("top_ready")
        gathered = [sem(f"gathered{j}") for j in range(UB)]
        index_ready = sem("index_ready")
        gather_begun = sem("gather_begun")
        et_put = sem("et_put")
        et_ready = sem("et_ready")
        q_done = sem("q_done")
        q_used = sem("q_used")
        var_summed = sem("var_summed")
        var_ready = sem("var_ready")
        sd_ready = sem("sd_ready")
        rs_ready = sem("rs_ready")
        rows_ready = sem("rows_ready")
        u_done = sem("u_done")
        ut_ready = sem("ut_ready")
        y_done = sem("y_done")
        sq_ready = sem("sq_ready")
        y_summed = sem("y_summed")
        y_sd_ready = sem("y_sd_ready")
        y_rs_ready = sem("y_rs_ready")
        y_ready = sem("y_ready")
        z_done = sem("z_done")
        zs_ready = sem("zs_ready")
        z_stored = [sem(f"z_stored{m}") for m in range(2)]
        dense_x_in = sem("dense_x_in")
        dense_m_in = sem("dense_m_in")
        dt_put = sem("dt_put")
        dt_ready = sem("dt_ready")
        x_done = sem("x_done")
        x_chain = sem("x_chain")
        x_var_ready = sem("x_var_ready")
        x_sd_ready = sem("x_sd_ready")
        x_ready = sem("x_ready")
        xt_done = sem("xt_done")
        xt_ready = sem("xt_ready")
        zb_in = sem("zb_in")
        read_begun = sem("read_begun")
        sum_put = sem("sum_put")
        zt_done = sem("zt_done")
        zt_ready = sem("zt_ready")
        pack_done = sem("pack_done")
        pack_ready = sem("pack_ready")
        l_done = sem("l_done")
        l_stat_ready = sem("l_stat_ready")
        l_var_ready = sem("l_var_ready")
        l_sd_ready = sem("l_sd_ready")
        l_rs_ready = sem("l_rs_ready")
        z_hat_ready = sem("z_hat_ready")
        hz_done = sem("hz_done")
        hz_ready = sem("hz_ready")
        h1_done = sem("h1_done")
        h1_ready = sem("h1_ready")
        h2_done = sem("h2_done")
        h2_ready = sem("h2_ready")
        out_done = sem("out_done")
        out_ready = sem("out_ready")
        out_stored = sem("out_stored")

        def after(eng, semaphore, count):
            if not isinstance(count, int) or count > 0:
                eng.wait_ge(semaphore, count)

        def stages(n):
            return n < NB, 1 <= n <= NB, 2 <= n

        def iterations(eng, body):
            body(0, 0)
            body(1, 1)
            with eng.Fori(2, NB) as i:
                body(i, 2)
            body(NB, NB)
            body(NB + 1, NB + 1)

        def present(n, j):
            units, layer, _ = stages(n)
            return units, (layer if j < 1 else units), (layer if j < 2 else units)

        N_FIRST, N_X, N_TOP = 5, 3, 10
        block = ctx.enter_context(nc.Block())

        @block.sync
        def _(sp):
            sp.dma_start(ids[:], a["ids"].rearrange("(t g s) f -> g t (s f)", g=128, s=SQ)).then_inc(ids_in, 16)
            sp.dma_start(eye[:], a["eye"]).then_inc(eye_in, 16)
            sp.dma_start(row_base[:], a["row_base"]).then_inc(eye_in, 16)
            sp.dma_start(ws[:], a["Ws"]).then_inc(first_in, 16)
            sp.dma_start(centre[:], a["centre"]).then_inc(first_in, 16)
            sp.dma_start(gs_bs[:], a["gs_bs"]).then_inc(first_in, 16)
            sp.dma_start(wsi[:], a["Wsi_blocks"]).then_inc(first_in, 16)
            sp.dma_start(last_one[:], a["last_one"]).then_inc(first_in, 16)

            dense = a["dense"].rearrange("(n g s) d -> n s g d", g=GB, s=SQ)

            def body(i, n):
                units, layer, top = stages(n)
                if units:
                    after(sp, dt_put, i)
                    for s in range(SQ):
                        sp.dma_start(dense_x[32 * s:32 * s + 32, :], dense[i, s]).then_inc(dense_x_in, 16)
                if n == 0:
                    sp.dma_start(wd[:], a["WdT"].rearrange("(c p) e -> p c e", p=128)).then_inc(x_weights_in, 16)
                    sp.dma_start(gd_b[:], a["gd_rows"]).then_inc(x_weights_in, 16)
                    sp.dma_start(bd_b[:], a["bd_rows"]).then_inc(x_weights_in, 16)
                    sp.dma_start(w1z[:], a["W1"][0:USED, :].rearrange("(c p) m -> p c m", p=128)).then_inc(top_weights_in, 16)
                    sp.dma_start(gl_bl[:], a["gl_bl"]).then_inc(top_weights_in, 16)
                    sp.dma_start(b1[:], a["b1"]).then_inc(top_weights_in, 16)
                    sp.dma_start(pair_gb[:], a["pair_gb"]).then_inc(top_weights_in, 16)
                    sp.dma_start(masks[:], a["masks"]).then_inc(top_weights_in, 16)
                    sp.dma_start(wl[:], a["Wl_rows"].rearrange("(c p) m -> p c m", p=128)).then_inc(top_weights_in, 16)
                    sp.dma_start(w1[:, 3:5, :], a["W1"][ML:ML + DD, :].rearrange("(c p) m -> p c m", p=128)
                                 ).then_inc(top_weights_in, 16)
                    sp.dma_start(w2[:], a["W2"].rearrange("(c p) m -> p c m", p=128)).then_inc(top_weights_in, 16)
                    sp.dma_start(b2[:], a["b2"]).then_inc(top_weights_in, 16)
                    sp.dma_start(w3[:], a["W3"]).then_inc(top_weights_in, 16)
                if top:
                    after(sp, dt_put, i)
                    for s in range(SQ):
                        sp.dma_start(dense_m[32 * s:32 * s + 32, :], dense[i - 2, s]).then_inc(dense_m_in, 16)
                for j in range(UB):
                    if present(n, j)[2]:
                        of, quarter = (i - 1 if j < 2 else i), (j - 2) % UB
                        sp.wait_ge(zs_ready, UB * i + j - 1)
                        sp.dma_start(scratch[of, :, GU * quarter:GU * quarter + GU, :],
                                     zs[:, j % 2]).then_inc(z_stored[j % 2], 16)
                    if j == 1 and layer:
                        for m in range(2):
                            sp.wait_ge(z_stored[m], 32 * i)
                        sp.sem_inc(read_begun, 1)
                        for s in range(SQ):
                            sp.dma_start(plain[32 * s:32 * s + 32],
                                         scratch[i - 1, 32 * s:32 * s + 32, :, :].rearrange("p g c -> g p c")
                                         ).then_inc(zb_in, 16)

            iterations(sp, body)
            sp.wait_ge(out_ready, NB)
            sp.dma_start(a["out"].rearrange("(a b) c -> a (b c)", a=1),
                         y_row[:].rearrange("p n g s -> p (n g s)")).then_inc(out_stored, 16)
            sp.wait_ge(out_stored, 16)

        @block.gpsimd
        def _(pool):
            def body(i):
                for j in range(UB):
                    pool.wait_ge(index_ready, UB * i + j + 1)
                    pool.sem_inc(gather_begun, 1)
                    for g in range(GU):
                        pool.indirect_dma_start(
                            out=rows[:, j, g, :], out_offset=None, in_=a["table"],
                            in_offset=bass.IndirectOffsetOnAxis(ap=index_now[:, j, g:g + 1], axis=0),
                        ).then_inc(gathered[j], 16)
            body(0)
            with pool.Fori(1, NB) as i:
                body(i)

        @block.tensor
        def _(pe):
            pe.wait_ge(eye_in, 32)
            pe.wait_ge(ids_float, 1)
            for t in range(4):
                last = nc.tensor.transpose(p_a[0:ROWS, 128 * t:128 * t + 128], ids_f[:, t, :], eye[:])
            last.then_inc(ids_turned, 1)
            pe.wait_ge(first_in, 16 * N_FIRST)
            nc.tensor.matmul(p_b[:, 0:D], centre[:], ws[:], start=True, stop=True).then_inc(wc_done, 1)
            pe.wait_ge(wc_ready, 2)
            nc.tensor.transpose(p_t[0:D + 1, 0:E], wc_gs[:], eye[:])
            nc.tensor.matmul(p_q[0:D, 0:D], wc[:], wc[:], start=True, stop=True)
            nc.tensor.matmul(p_q[D:2 * D, 0:D], wc[:], wc[:], start=True, stop=True).then_inc(wy_done, 1)
            pe.wait_ge(wsi_ready, 1)
            nc.tensor.matmul(p_u[0:D + 1, 0:SQ * NP], last_one[:], wsi_c[:].rearrange("r s p -> r (s p)"),
                             start=True, stop=True).then_inc(u_const_done, 1)
            pe.wait_ge(units_ready, 1)

            def body(i, n):
                units, layer, top = stages(n)
                for j in range(UB):
                    k = UB * i + j
                    now, lag1, lag2 = present(n, j)
                    if now:
                        pe.wait_ge(gathered[j], 16 * GU * (i + 1))
                        after(pe, et_ready, k)
                        for m in range(GU // 2):
                            last = nc.tensor.transpose(
                                p_t[:, ROWS * m:ROWS * m + ROWS],
                                rows[:, j, 2 * m:2 * m + 2, :].rearrange("r g d -> r (g d)"), eye[0:ROWS, 0:ROWS])
                        last.then_inc(et_put, 1)
                    if j == 0 and (units or top):
                        after(pe, zt_ready, i - 1)
                        if units:
                            pe.wait_ge(dense_x_in, 64 * (i + 1))
                            for c in range(2):
                                last = nc.tensor.transpose(p_a[:, 128 * c:128 * c + 128],
                                                           dense_x[:, 128 * c:128 * c + 128], eye[:])
                        if top:
                            pe.wait_ge(dense_m_in, 64 * (i - 1))
                            for c in range(2):
                                last = nc.tensor.transpose(p_a[:, 256 + 128 * c:384 + 128 * c],
                                                           dense_m[:, 128 * c:128 * c + 128], eye[:])
                        last.then_inc(dt_put, 1)
                    if lag1:
                        pe.wait_ge(rows_ready, k)
                        after(pe, ut_ready, 2 * (k - 1))
                        for g in range(GU):
                            h = g % 2
                            last = nc.tensor.matmul(p_u[D * h:D * h + D, 128 * (g // 2):128 * (g // 2) + 128],
                                                    rows_n[:, g, :], wsi_c[:].rearrange("r s p -> r (s p)"),
                                                    start=True, stop=True)
                        last.then_inc(u_done, 1)
                    if now:
                        pe.wait_ge(et_ready, k + 1)
                        after(pe, q_used, k)
                        for m in range(GU // 2):
                            last = nc.tensor.matmul(p_q[0:ROWS, 128 * m:128 * m + 128], et[:, m, :], gram[:],
                                                    start=True, stop=True)
                        last.then_inc(q_done, 1)
                    if lag2:
                        pe.wait_ge(y_ready, k - 1)
                        pe.wait_ge(xt_ready, i if j < 2 else i + 1)
                        after(pe, zs_ready, k - 2)
                        for g in range(GU):
                            for s in range(SQ):
                                f = feat[:, (j - 2) % UB, SQ * g + s, :]
                                last = nc.tensor.matmul(p_z[32 * s:32 * s + 32, SLOTS * g:SLOTS * g + SLOTS],
                                                        f[:, 2:SLOTS], f, start=True, stop=True)
                        last.then_inc(z_done, 1)
                    if j == 0 and units:
                        pe.wait_ge(dt_ready, i + 1)
                        pe.wait_ge(x_weights_in, 16 * N_X)
                        for c in range(2):
                            last = nc.tensor.matmul(p_a[:, 0:E], dt[:, c, :], wd[:, c, :], start=c == 0, stop=c == 1)
                        last.then_inc(x_done, 1)
                    if j == 0 and top:
                        pe.wait_ge(z_hat_ready, i - 1)
                        for c in range(3):
                            last = nc.tensor.transpose(p_b[:, 128 * c:128 * c + 128],
                                                       z_hat[:, 128 * c:128 * c + 128], eye[:])
                        last.then_inc(hz_done, 1)
                    if j == 1 and units:
                        pe.wait_ge(x_ready, i + 1)
                        nc.tensor.transpose(p_a[:, 128:256], x_full[:], eye[:]).then_inc(xt_done, 1)
                    if j == 2 and top:
                        pe.wait_ge(h2_ready, 2 * (i - 1))
                        for c in range(2):
                            last = nc.tensor.matmul(p_b[0:1, 256:384], w3[:, c:c + 1], h2[:, c, :],
                                                    start=c == 0, stop=c == 1)
                        last.then_inc(out_done, 1)
                    if lag1:
                        pe.wait_ge(ut_ready, 2 * k)
                        after(pe, y_ready, k - 1)
                        for h in range(2):
                            last = nc.tensor.matmul(p_y[:, 512 * h:512 * h + 512], wy[:],
                                                    ut[:, 4 * h:4 * h + 4, :].rearrange("d g c -> d (g c)"),
                                                    start=True, stop=True)
                        last.then_inc(y_done, 1)
                    if n == 0 and j == 2:
                        pe.wait_ge(top_weights_in, 16 * N_TOP)
                        for m in range(4):
                            for c in range(3):
                                last = nc.tensor.matmul(p_b[:, 128 + m:129 + m], w1z[:, c, 128 * m:128 * m + 128],
                                                        gl_bl[:, 1, c:c + 1], start=c == 0, stop=c == 2)
                        last.then_inc(bl_done, 1)
                    if n == 1 and j == 0:
                        pe.wait_ge(fold_ready, 1)
                        for c in range(KC):
                            last = nc.tensor.matmul(p_b[:], fold[:, c, :], wl[:, c, :], start=c == 0, stop=c == KC - 1)
                        last.then_inc(fold_done, 1)
                    if j == 0 and top:
                        pe.wait_ge(dt_ready, i + 1)
                        pe.wait_ge(hz_ready, i - 1)
                        for m in range(4):
                            for c in range(5):
                                last = nc.tensor.matmul(p_b[:, 128 * m:128 * m + 128],
                                                        w1[:, c, 128 * m:128 * m + 128],
                                                        hz[:, c, :] if c < 3 else dt[:, c - 1, :],
                                                        start=c == 0, stop=c == 4)
                        last.then_inc(h1_done, 1)
                    if j == 1 and top:
                        pe.wait_ge(h1_ready, 4 * (i - 1))
                        for m in range(2):
                            for c in range(4):
                                last = nc.tensor.matmul(p_b[:, 128 * m:128 * m + 128],
                                                        w2[:, c, 128 * m:128 * m + 128], h1[:, c, :],
                                                        start=c == 0, stop=c == 3)
                        last.then_inc(h2_done, 1)
                    if j == 2 and layer:
                        if n == 1:
                            pe.wait_ge(top_ready, 1)
                        pe.wait_ge(zb_in, 64 * i)
                        if units:
                            pe.wait_ge(xt_ready, i + 1)
                        for k4 in range(16):
                            q = k4 % 4
                            last = nc.tensor.matmul(p_a[32 * q:32 * q + 32, 32 * (k4 - q):32 * (k4 - q) + 128],
                                                    skew[:, :, k4], eye[:], start=True, stop=True)
                        last.then_inc(zt_done, 1)
                        pe.wait_ge(sum_put, i)
                        after(pe, out_ready, i - 1)
                        for q, products in enumerate((skew[:, :, 16], skew[:, :, 17], plain[:, :, 1], plain[:, :, 0])):
                            last = nc.tensor.matmul(p_b[32 * q:32 * q + 32, PACK:PACK + 128], products, eye[:],
                                                    start=True, stop=True)
                        last.then_inc(pack_done, 1)
                    if j == 3 and layer:
                        pe.wait_ge(zt_ready, i)
                        pe.wait_ge(pack_ready, i)
                        for c in range(KC):
                            last = nc.tensor.matmul(p_b[:], zt[:, c, :], wk[:, c, :], start=c == 0, stop=c == KC - 1)
                        last.then_inc(l_done, 1)

            iterations(pe, body)

        @block.scalar
        def _(act):
            act.wait_ge(units_ready, 1)

            def body(i, n):
                units, layer, top = stages(n)
                for j in range(UB):
                    k = UB * i + j
                    now, lag1, lag2 = present(n, j)
                    if now:
                        act.wait_ge(et_put, k + 1)
                        after(act, q_done, k)
                        nc.scalar.copy(et[:].rearrange("d m r -> d (m r)"), p_t[:, 0:ROWS * GU // 2]).then_inc(et_ready, 1)
                    if j == 0 and top:
                        act.wait_ge(l_var_ready, i - 1)
                        nc.scalar.activation(l_sd[:], l_mv[:, 1:2], ACT.Sqrt, bias=eps_col[:]).then_inc(l_sd_ready, 1)
                    if lag1:
                        act.wait_ge(u_done, k)
                        after(act, y_done, k - 1)
                        for h in range(2):
                            nc.scalar.copy(ut[0:D, :, :].rearrange("d (g h) c -> d h g c", h=2)[:, h],
                                           p_u[D * h:D * h + D, :].rearrange("d (g c) -> d g c", g=GU // 2)
                                           ).then_inc(ut_ready, 1)
                    if j == 0 and (units or top):
                        lo, hi = (0 if units else 2), (4 if top else 2)
                        act.wait_ge(dt_put, i + 1)
                        after(act, x_done, i if units else NB)
                        after(act, h1_done, i - 2)
                        nc.scalar.copy(dt[:, lo:hi, :].rearrange("d c b -> d (c b)"),
                                       p_a[:, 128 * lo:128 * hi]).then_inc(dt_ready, 1)
                    if j == 1 and top:
                        act.wait_ge(h1_done, i - 1)
                        after(act, h2_done, i - 2)
                        for m in range(4):
                            nc.scalar.activation(h1[:, m, :], p_b[:, 128 * m:128 * m + 128], ACT.Relu,
                                                 bias=b1z[:, m:m + 1]).then_inc(h1_ready, 1)
                    if j == 2 and top:
                        act.wait_ge(h2_done, i - 1)
                        after(act, out_done, i - 2)
                        for m in range(2):
                            nc.scalar.activation(h2[:, m, :], p_b[:, 128 * m:128 * m + 128], ACT.Relu,
                                                 bias=b2[:, m:m + 1]).then_inc(h2_ready, 1)
                    if lag2:
                        act.wait_ge(z_done, k - 1)
                        after(act, z_stored[j % 2], 16 * (2 * i + (j - 2) // 2))
                        nc.scalar.copy(zs[:, j % 2].rearrange("r g c -> r (g c)"), p_z[:, 0:GU * SLOTS]).then_inc(zs_ready, 1)
                    if j == 1 and units:
                        act.wait_ge(xt_done, i + 1)
                        after(act, z_done, UB * i)
                        nc.scalar.copy(feat[:].rearrange("e u (g s) c -> e c s (u g)", s=SQ)[:, 0],
                                       p_a[:, 128:256].rearrange("e (s g) -> e s g", s=SQ)).then_inc(xt_ready, 1)
                    if j == 0 and top:
                        act.wait_ge(hz_done, i - 1)
                        nc.scalar.copy(hz[:].rearrange("d c b -> d (c b)"), p_b[:, 0:USED]).then_inc(hz_ready, 1)
                    if now:
                        act.wait_ge(var_ready, k + 1)
                        nc.scalar.activation(sd_e[:], var_g[:], ACT.Sqrt).then_inc(sd_ready, 1)
                    if j == 0 and units:
                        act.wait_ge(x_var_ready, i + 1)
                        nc.scalar.activation(x_sd[:], x_mv[:, 1:2], ACT.Sqrt, bias=eps_col[:]).then_inc(x_sd_ready, 1)
                    if j == 2 and top:
                        act.wait_ge(out_done, i - 1)
                        nc.scalar.copy(y_row[:, i - 2, :, :].rearrange("p g s -> p s g"),
                                       p_b[0:1, 256:384].rearrange("p (s g) -> p s g", s=SQ)).then_inc(out_ready, 1)
                    if lag1:
                        act.wait_ge(y_done, k)
                        after(act, y_summed, k - 1)
                        nc.scalar.activation(y_sq[:].rearrange("e b p -> e (b p)"), p_y[:], ACT.Square).then_inc(sq_ready, 1)
                        act.wait_ge(y_summed, k)
                        nc.scalar.activation(y_sd[:], y_sum[:], ACT.Sqrt, bias=eps_col[:], scale=1.0 / NP).then_inc(y_sd_ready, 1)
                    if j == 2 and layer:
                        act.wait_ge(zt_done, i)
                        after(act, l_done, i - 1)
                        nc.scalar.copy(zt[:, 0:4, :].rearrange("r c b -> r (c b)"), p_a[:]).then_inc(zt_ready, 1)
                    if n == 1 and j == 3:
                        act.wait_ge(top_ready, 1)

            iterations(act, body)

        @block.vector
        def _(dve):
            dve.wait_ge(ids_in, 16)
            nc.vector.tensor_copy(ids_f[:], ids[:]).then_inc(ids_float, 1)
            nc.vector.memset(index[:, NG:], 0).then_inc(prepared, 1)
            nc.vector.memset(eps_col[:], EPS).then_inc(prepared, 1)
            nc.vector.memset(gram[:], 0.0).then_inc(prepared, 1)
            dve.wait_ge(ids_turned, 1)
            nc.vector.tensor_scalar(index[:, 0:NG], p_a[0:ROWS, :], row_base[:], None, ALU.add).then_inc(prepared, 1)
            dve.wait_ge(prepared, 4)
            for j in range(UB):
                nc.vector.tensor_copy(index_now[:, j, :], index[:, GU * j:GU * j + GU]).then_inc(index_ready, 1)
            dve.wait_ge(wc_done, 1)
            nc.vector.tensor_copy(wc[:], p_b[:, 0:D]).then_inc(wc_ready, 1)
            nc.vector.tensor_copy(wc_gs[:, D:D + 1], gs_bs[:, 1:2]).then_inc(prepared, 1)
            dve.wait_ge(prepared, 5)
            nc.vector.tensor_scalar(wc_gs[:, 0:D], p_b[:, 0:D], gs_bs[:, 0:1], None, ALU.mult).then_inc(wc_ready, 1)
            nc.vector.tensor_reduce(wsi_sum[:], wsi[:], AX, ALU.add).then_inc(prepared, 1)
            dve.wait_ge(prepared, 6)
            nc.vector.scalar_tensor_tensor(out=wsi_c[:], in0=wsi_sum[:].unsqueeze(2).to_broadcast([ROWS, SQ, NP]),
                                           scalar=-1.0 / NP, in1=wsi[:], op0=ALU.mult, op1=ALU.add).then_inc(wsi_ready, 1)
            nc.vector.memset(feat[:, :, :, 1], 1.0).then_inc(prepared, 1)
            nc.vector.memset(zb[:], 0.0).then_inc(prepared, 1)
            dve.wait_ge(wy_done, 1)
            nc.vector.tensor_copy(wy[:], p_t[0:D + 1, 0:E]).then_inc(prepared, 1)
            for h in range(2):
                nc.vector.tensor_scalar(gram[D * h:D * h + D, D * h:D * h + D], p_q[D * h:D * h + D, 0:D], 1.0 / E,
                                        None, ALU.mult).then_inc(prepared, 1)
            dve.wait_ge(u_const_done, 1)
            nc.vector.tensor_copy(ut[D:D + 1, :, :], p_u[D:D + 1, 0:SQ * NP].unsqueeze(1).to_broadcast([1, GU, SQ * NP])
                                  ).then_inc(prepared, 1)
            dve.wait_ge(prepared, 12)
            nc.vector.sem_inc(units_ready, 1)

            def prepare_layers(part):
                if part == 0:
                    dve.wait_ge(top_weights_in, 16 * N_TOP)
                    for c in range(3):
                        nc.vector.tensor_scalar(w1[:, c, :], w1z[:, c, :], gl_bl[:, 0, c:c + 1], None, ALU.mult
                                                ).then_inc(prepared, 1)
                    for n, (u, v) in enumerate(((0, 1), (0, 3), (1, 2), (2, 3))):
                        nc.vector.tensor_tensor(pair_x[:, n, :], pair_gb[:, u, :], pair_gb[:, v, :], ALU.mult
                                                ).then_inc(prepared, 1)
                elif part == 1:
                    dve.wait_ge(prepared, 19)
                    for c in range(KC):
                        nc.vector.tensor_scalar(fold[:, c, :], masks[:, 0, c, :], pair_x[:, 1, c:c + 1], None, ALU.mult
                                                ).then_inc(prepared, 1)
                    for c in range(KC):
                        nc.vector.tensor_scalar(wk[:, c, :], wl[:, c, :], pair_x[:, 0, c:c + 1], None, ALU.mult
                                                ).then_inc(prepared, 1)
                elif part == 2:
                    for m in (1, 2):
                        dve.wait_ge(prepared, 24 + KC * m)
                        for c in range(KC):
                            nc.vector.scalar_tensor_tensor(
                                out=fold[:, c, :], in0=masks[:, m, c, :], scalar=pair_x[:, m + 1, c:c + 1],
                                in1=fold[:, c, :], op0=ALU.mult, op1=ALU.add).then_inc(prepared, 1)
                    dve.wait_ge(bl_done, 1)
                    nc.vector.tensor_tensor(b1z[:], p_b[:, 128:132], b1[:], ALU.add).then_inc(prepared, 1)
                    nc.vector.memset(skew[:, NP - 1:NP, 17], 1.0).then_inc(prepared, 1)
                    dve.wait_ge(prepared, 41)
                    nc.vector.sem_inc(fold_ready, 1)
                else:
                    dve.wait_ge(fold_done, 1)
                    nc.vector.tensor_tensor(wk[:, KC - 1, :], wk[:, KC - 1, :], p_b[:], ALU.add).then_inc(top_ready, 1)

            def body(i, n):
                units, layer, top = stages(n)
                for j in range(UB):
                    k = UB * i + j
                    now, lag1, _ = present(n, j)
                    if j == 0 and top:
                        dve.wait_ge(l_done, i - 1)
                        nc.vector.bn_stats(l_stat[:], p_b[:]).then_inc(l_stat_ready, 1)
                        dve.wait_ge(top_weights_in, 16 * N_TOP)
                        dve.wait_ge(l_stat_ready, i - 1)
                        nc.vector.bn_aggr(l_mv[:], l_stat[:]).then_inc(l_var_ready, 1)
                        dve.wait_ge(l_sd_ready, i - 1)
                        nc.vector.reciprocal(l_rs[:], l_sd[:]).then_inc(l_rs_ready, 1)
                        dve.wait_ge(l_rs_ready, i - 1)
                        nc.vector.tensor_scalar(z_hat[:], p_b[:, 0:USED], l_mv[:, 0:1], l_rs[:], ALU.subtract, ALU.mult
                                                ).then_inc(z_hat_ready, 1)
                    if now:
                        dve.wait_ge(q_done, k + 1)
                        nc.vector.tensor_tensor(prod[:].rearrange("r g d -> r (g d)"), p_q[0:ROWS, :],
                                                rows[:, j, :, :].rearrange("r g d -> r (g d)"), ALU.mult).then_inc(q_used, 1)
                        dve.wait_ge(q_used, k + 1)
                        nc.vector.tensor_reduce(var_e[:], prod[:], AX, ALU.add).then_inc(var_summed, 1)
                        dve.wait_ge(var_summed, k + 1)
                        nc.vector.tensor_scalar(var_g[:], var_e[:], 0.0, EPS, ALU.max, ALU.add).then_inc(var_ready, 1)
                        dve.wait_ge(sd_ready, k + 1)
                        nc.vector.reciprocal(rs_e[:], sd_e[:]).then_inc(rs_ready, 1)
                        dve.wait_ge(rs_ready, k + 1)
                        after(dve, u_done, k)
                        nc.vector.tensor_tensor(rows_n[:], rows[:, j, :, :], rs_e[:].unsqueeze(2).to_broadcast([ROWS, GU, D]),
                                                ALU.mult).then_inc(rows_ready, 1)
                        nc.vector.tensor_copy(index_now[:, j, :], index[:, bass.ds(GU * (k + UB), GU)]).then_inc(index_ready, 1)
                    if j == 0 and units:
                        dve.wait_ge(x_done, i + 1)
                        nc.vector.bn_stats(x_stat[:], p_a[:, 0:E]).then_inc(x_chain, 1)
                        dve.wait_ge(x_weights_in, 16 * N_X)
                        dve.wait_ge(x_chain, 4 * i + 1)
                        nc.vector.bn_aggr(x_mv[:], x_stat[:]).then_inc(x_var_ready, 1)
                        dve.wait_ge(x_sd_ready, i + 1)
                        nc.vector.reciprocal(x_rs[:], x_sd[:]).then_inc(x_chain, 1)
                        dve.wait_ge(x_chain, 4 * i + 2)
                        nc.vector.tensor_scalar(x_hat[:], p_a[:, 0:E], x_mv[:, 0:1], x_rs[:], ALU.subtract, ALU.mult
                                                ).then_inc(x_chain, 1)
                        dve.wait_ge(x_chain, 4 * i + 3)
                        nc.vector.tensor_tensor(x_g[:], x_hat[:], gd_b[:], ALU.mult).then_inc(x_chain, 1)
                        dve.wait_ge(x_chain, 4 * i + 4)
                        nc.vector.tensor_tensor(x_full[:], x_g[:], bd_b[:], ALU.add).then_inc(x_ready, 1)
                    if lag1:
                        dve.wait_ge(sq_ready, k)
                        nc.vector.tensor_reduce(y_sum[:], y_sq[:], AX, ALU.add).then_inc(y_summed, 1)
                        dve.wait_ge(y_sd_ready, k)
                        nc.vector.reciprocal(y_rs[:], y_sd[:]).then_inc(y_rs_ready, 1)
                        dve.wait_ge(y_rs_ready, k)
                        after(dve, z_done, k - UB)
                        nc.vector.tensor_tensor(feat[:, (j - 1) % UB, :, 2:SLOTS], p_y[:].rearrange("e (b p) -> e b p", p=NP),
                                                y_rs[:].unsqueeze(2).to_broadcast([E, SU, NP]), ALU.mult).then_inc(y_ready, 1)
                    if j == 2 and layer:
                        dve.wait_ge(pack_done, i)
                        after(dve, l_done, i - 1)
                        nc.vector.tensor_copy(zt[:, KC - 1, :], p_b[:, PACK:PACK + 128]).then_inc(pack_ready, 1)
                    if j == 3 and units:
                        after(dve, pack_done, i)
                        nc.vector.tensor_reduce(skew[:, NP - 1:NP, 16], x_full[:], AX, ALU.add).then_inc(sum_put, 1)
                    if n == 0 and j >= 1:
                        prepare_layers(j - 1)
                    if n == 1 and j == 0:
                        prepare_layers(3)

            iterations(dve, body)


_TABLES = [f"tbl_{f}" for f in range(NF)]


def kernel(**inputs):
    import concourse.bacc as _bacc
    from concourse.bass_utils import run_bass_kernel_spmd as _run

    x = {k: np.asarray(v) for k, v in inputs.items()}
    pairs = interaction_rows()
    wl_cols = np.concatenate([x["L0_rec_Wl"].T, np.zeros((1, ML), np.float32)])
    first = np.array([r[1] for r in pairs]).reshape(KC, 128).T
    second = np.array([r[2] for r in pairs]).reshape(KC, 128).T
    gsi = np.concatenate([x["L0_rec_gsi"], np.array([1.0, 0.0], np.float32)])
    bsi = np.concatenate([x["L0_rec_bsi"], np.array([0.0, 0.0], np.float32)])
    wsi_blocks = np.zeros((SQ, NF, SQ, NP), np.float32)
    for s in range(SQ):
        wsi_blocks[s, :, s, :] = x["L0_rec_Wsi"].T
    masks = np.zeros((3, KC * 128, 128), np.float32)
    for n, (col, p, q) in enumerate(pairs):
        if col < 0:
            continue
        if q < NP:
            masks[0, n, COL_ONES + p] = 1.0
            masks[1, n, COL_ONES + q] = 1.0
            masks[2, n, COL_ONE] = float(E)
        else:
            masks[1, n, COL_SUM] = 1.0
    last_one = np.zeros((ROWS, D + 1), np.float32)
    last_one[:, D] = 1.0
    base = np.concatenate([[0], np.cumsum(VOCAB)[:-1]]).astype(np.float32)

    def cols(v):
        return v.reshape(-1, 128).T

    arrays = {
        "ids": x["ids"],
        "table": np.concatenate([x[t] for t in _TABLES]),
        "dense": x["r_dense_t"],
        "Ws": x["L0_rec_Ws"],
        "gs_bs": np.stack([x["L0_rec_gs"], x["L0_rec_bs"]], 1),
        "Wsi_blocks": wsi_blocks.reshape(ROWS, SQ, NP),
        "WdT": x["L0_rec_Wd"].T,
        "gd_rows": np.broadcast_to(x["L0_rec_gd"], (128, E)),
        "bd_rows": np.broadcast_to(x["L0_rec_bd"], (128, E)),
        "Wl_rows": wl_cols[[r[0] for r in pairs]],
        "pair_gb": np.stack([gsi[first], gsi[second], bsi[first], bsi[second]], 1),
        "W1": x["W_top1"],
        "gl_bl": np.stack([cols(x["L0_rec_gl"][:USED]), cols(x["L0_rec_bl"][:USED])], 1),
        "b1": cols(x["b_top1"]),
        "W2": x["W_top2"],
        "b2": cols(x["b_top2"]),
        "W3": x["W_top3"].reshape(2, 128).T,
        "eye": np.eye(128, dtype=np.float32),
        "centre": (np.eye(E) - 1.0 / E).astype(np.float32),
        "masks": masks.reshape(3, KC, 128, 128).transpose(2, 0, 1, 3),
        "last_one": last_one,
        "row_base": np.tile(base, SQ).reshape(ROWS, 1),
    }
    arrays = {k: np.ascontiguousarray(v) for k, v in arrays.items()}
    nc = _bacc.Bacc("TRN2", target_bir_lowering=False, num_devices=1)
    a = {k: nc.dram_tensor(f"in_{k}", v.shape, mybir.dt.from_np(v.dtype), kind="ExternalInput").ap()
         for k, v in arrays.items()}
    a["out"] = nc.dram_tensor("out_y", (B, 1), F32, kind="ExternalOutput").ap()
    dlrm_kernel(nc, a)
    r = _run(nc, [{f"in_{k}": v for k, v in arrays.items()}], core_ids=[0])
    return r.results[0]["out_y"]
```

```python
from contextlib import ExitStack

import numpy as np

import concourse.bass as bass
from concourse import mybir

F32 = mybir.dt.float32
F32R = mybir.dt.float32r
I32 = mybir.dt.int32
ALU = mybir.AluOpType
ACT = mybir.ActivationFunctionType
AX = mybir.AxisListType.X

EPS = 1e-5
VOCAB = [1000, 1000, 1000, 125000, 12500, 12500, 12500, 1000, 12500, 12500, 1000, 125000, 125000,
         12500, 12500, 1000, 1250, 12500, 1000, 1000, 1250, 1000, 1000, 1250, 1000, 1250]
B = 2048
NF = len(VOCAB)
D = 64
E = 128
NP = 32
DD = 256
ML = 512
USED = 384
H1, H2 = 512, 256

SQ = 4
ROWS = SQ * NF
GU = 8
SU = SQ * GU
UB = 4
SB = UB * SU
GB = UB * GU
NB = B // SB
NG = B // SQ
SLOTS = NP + 2
KC = 5
NK = 18
ZROW = NP * SLOTS
PACK = 384
ZPAD = 3 + NP * (SLOTS + 1)

COL_SUM, COL_ONE, COL_ONES = 31, 63, 64


def pair_at(p, k):
    row, slot = divmod(p * SLOTS + 2 + p + k, SLOTS)
    if row >= NP or slot < 2 or slot - 2 == row:
        return None
    return max(row, slot - 2), min(row, slot - 2)


def interaction_rows():
    at = [pair_at(p, k + 1) for k in range(NK) for p in range(NP)]
    taken, rows = set(), []
    for pair in at:
        if pair is None or pair in taken:
            rows.append((-1, NP + 1, NP + 1))
            continue
        taken.add(pair)
        i, j = pair[0] + 1, pair[1] + 1
        rows.append((i * (i - 1) // 2 + j, pair[0], pair[1]))
    rows += [(-1, NP + 1, NP + 1)] * NP
    rows += [((p + 1) * p // 2, p, NP) for p in range(NP)]
    assert len(taken) == NP * (NP - 1) // 2 and len(rows) == KC * 128
    return rows


def dlrm_kernel(nc, a):
    scratch = nc.dram_tensor("products", (NB, 128, GB, SLOTS), F32, kind="Internal").ap()
    with ExitStack() as ctx:
        def sb(name, shape, dt=F32):
            return ctx.enter_context(nc.sbuf_tensor(name, shape, dt))

        def pb(name):
            return ctx.enter_context(nc.psum_tensor(name, [128, 512], F32))

        def sem(name):
            return ctx.enter_context(nc.semaphore(name))

        eye = sb("eye", [128, 128])
        centre = sb("centre", [128, 128])
        masks = sb("masks", [128, 3, KC, 128])
        row_base = sb("row_base", [ROWS, 1])
        last_one = sb("last_one", [ROWS, D + 1])
        ws = sb("ws", [E, D])
        gs_bs = sb("gs_bs", [E, 2])
        wc = sb("wc", [E, D])
        wc_gs = sb("wc_gs", [E, D + 1])
        wy = sb("wy", [D + 1, E])
        gram = sb("gram", [128, 128])
        wsi = sb("wsi", [ROWS, SQ, NP])
        wsi_sum = sb("wsi_sum", [ROWS, SQ])
        wsi_c = sb("wsi_c", [ROWS, SQ, NP])
        wd = sb("wd", [128, 2, E])
        gd_b = sb("gd_b", [128, E])
        bd_b = sb("bd_b", [128, E])
        w1z = sb("w1z", [128, 3, H1])
        w1 = sb("w1", [128, 5, H1])
        gl_bl = sb("gl_bl", [128, 2, 3])
        b1 = sb("b1", [128, 4])
        bl_w1 = sb("bl_w1", [128, 4])
        b1z = sb("b1z", [128, 4])
        w2 = sb("w2", [128, 4, H2])
        b2 = sb("b2", [128, 2])
        w3 = sb("w3", [128, 2])
        wl = sb("wl", [128, KC, ML])
        wk = sb("wk", [128, KC, ML])
        wk_high = sb("wk_high", [128, KC, ML], F32R)
        wk_low = sb("wk_low", [128, KC, ML], F32R)
        pair_gb = sb("pair_gb", [128, 4, KC])
        pair_x = sb("pair_x", [128, 4, KC])
        fold = sb("fold", [128, KC, 128])
        ids = sb("ids", [128, 4, ROWS], I32)
        ids_f = sb("ids_f", [128, 4, ROWS])
        index = sb("index", [ROWS, NG + UB * GU], I32)
        index_now = sb("index_now", [ROWS, UB, GU], I32)
        rows = sb("rows", [ROWS, UB, GU, D])
        et = sb("et", [128, GU // 2, ROWS])
        prod = sb("prod", [ROWS, GU, D])
        var_e = sb("var_e", [ROWS, GU])
        var_g = sb("var_g", [ROWS, GU])
        sd_e = sb("sd_e", [ROWS, GU])
        rs_e = sb("rs_e", [ROWS, GU])
        rows_n = sb("rows_n", [ROWS, GU, D])
        ut = sb("ut", [D + 1, GU, SQ * NP])
        y_sq = sb("y_sq", [E, SU, NP])
        y_sum = sb("y_sum", [E, SU])
        y_sd = sb("y_sd", [E, SU])
        y_rs = sb("y_rs", [E, SU])
        feat = sb("feat", [E, UB, SU, SLOTS])
        zs = sb("zs", [128, 2, GU, SLOTS])
        dense_x = sb("dense_x", [128, DD])
        dt = sb("dt", [128, 2, 128])
        dt_all = sb("dt_all", [128, NB, 2, 128])
        x_stat = sb("x_stat", [128, 6])
        x_mv = sb("x_mv", [128, 2])
        x_sd = sb("x_sd", [128, 1])
        x_rs = sb("x_rs", [128, 1])
        x_hat = sb("x_hat", [128, E])
        x_g = sb("x_g", [128, E])
        x_full = sb("x_full", [128, E])
        zb = sb("zb", [128, ZPAD])
        zt_high = sb("zt_high", [128, KC, 128], F32R)
        zt_low = sb("zt_low", [128, KC, 128], F32R)
        l_stat = sb("l_stat", [128, 6])
        l_mv = sb("l_mv", [128, 2])
        l_sd = sb("l_sd", [128, 1])
        l_rs = sb("l_rs", [128, 1])
        z_hat = sb("z_hat", [128, USED])
        hz = sb("hz", [128, 3, 128])
        h1 = sb("h1", [128, 4, 128])
        h2 = sb("h2", [128, 2, 128])
        y_row = sb("y_row", [1, NB, GB, SQ])
        eps_col = sb("eps_col", [128, 1])

        p_t, p_q, p_u, p_z, p_a, p_b = (pb(n) for n in ("p_t", "p_q", "p_u", "p_z", "p_a", "p_b"))
        p_y = ctx.enter_context(nc.psum_tensor("p_y", [128, 1024], F32))

        skew = zb[:, 3:3 + NP * (SLOTS + 1)].rearrange("b (p k) -> b p k", k=SLOTS + 1)
        plain = zb[:, 0:ZROW].rearrange("b (p c) -> b p c", c=SLOTS)

        ids_in = sem("ids_in")
        eye_in = sem("eye_in")
        base_in = sem("base_in")
        first_in = sem("first_in")
        fold_in = sem("fold_in")
        w1z_in = sem("w1z_in")
        wl_in = sem("wl_in")
        x_weights_in = sem("x_weights_in")
        top_weights_in = sem("top_weights_in")
        ids_float = sem("ids_float")
        ids_turned = sem("ids_turned")
        wc_done = sem("wc_done")
        wc_ready = sem("wc_ready")
        wy_done = sem("wy_done")
        wsi_ready = sem("wsi_ready")
        u_const_done = sem("u_const_done")
        prepared = sem("prepared")
        units_ready = sem("units_ready")
        table_loaded = sem("table_loaded")
        bl_done = sem("bl_done")
        bl_ready = sem("bl_ready")
        fold_ready = sem("fold_ready")
        fold_done = sem("fold_done")
        wk_ready = sem("wk_ready")
        wk_summed = sem("wk_summed")
        wk_high_ready = sem("wk_high_ready")
        top_ready = sem("top_ready")
        gathered = [sem(f"gathered{j}") for j in range(UB)]
        index_ready = sem("index_ready")
        gather_begun = sem("gather_begun")
        et_put = sem("et_put")
        et_ready = sem("et_ready")
        q_done = sem("q_done")
        q_used = sem("q_used")
        var_summed = sem("var_summed")
        var_ready = sem("var_ready")
        sd_ready = sem("sd_ready")
        rs_ready = sem("rs_ready")
        rows_ready = sem("rows_ready")
        u_done = sem("u_done")
        ut_ready = sem("ut_ready")
        y_done = sem("y_done")
        sq_ready = sem("sq_ready")
        y_summed = sem("y_summed")
        y_sd_ready = sem("y_sd_ready")
        y_rs_ready = sem("y_rs_ready")
        y_ready = sem("y_ready")
        z_done = sem("z_done")
        zs_ready = sem("zs_ready")
        z_stored = [sem(f"z_stored{m}") for m in range(2)]
        dense_x_in = sem("dense_x_in")
        dt_put = sem("dt_put")
        dt_ready = sem("dt_ready")
        x_done = sem("x_done")
        x_chain = sem("x_chain")
        x_var_ready = sem("x_var_ready")
        x_sd_ready = sem("x_sd_ready")
        x_ready = sem("x_ready")
        xt_done = sem("xt_done")
        xt_ready = sem("xt_ready")
        zb_in = sem("zb_in")
        read_begun = sem("read_begun")
        sum_put = sem("sum_put")
        zt_done = sem("zt_done")
        zt_ready = sem("zt_ready")
        zt_low_ready = sem("zt_low_ready")
        pack_done = sem("pack_done")
        pack_ready = sem("pack_ready")
        l_done = sem("l_done")
        l_stat_ready = sem("l_stat_ready")
        l_var_ready = sem("l_var_ready")
        l_sd_ready = sem("l_sd_ready")
        l_rs_ready = sem("l_rs_ready")
        z_hat_ready = sem("z_hat_ready")
        hz_done = sem("hz_done")
        hz_ready = sem("hz_ready")
        h1_done = sem("h1_done")
        h1_ready = sem("h1_ready")
        h2_done = sem("h2_done")
        h2_ready = sem("h2_ready")
        out_done = sem("out_done")
        out_ready = sem("out_ready")
        out_stored = sem("out_stored")

        def after(eng, semaphore, count):
            if not isinstance(count, int) or count > 0:
                eng.wait_ge(semaphore, count)

        def stages(n):
            return n < NB, 1 <= n <= NB, 2 <= n

        def iterations(eng, body, peel=False):
            body(0, 0)
            body(1, 1)
            with eng.Fori(2, NB - 1 if peel else NB) as i:
                body(i, 2)
            if peel:
                body(NB - 1, NB - 1)
            body(NB, NB)
            body(NB + 1, NB + 1)

        def present(n, j):
            units, layer, _ = stages(n)
            return units, (layer if j < 1 else units), (layer if j < 2 else units)

        CUT = (2, 1)
        PREPARATION = ((0, 1), (0, 2), (1, 0), (1, 1), (1, 2))
        FOLD = ((0, 1), (2,), (3, 4))
        assert [c for chunks in FOLD for c in chunks] == list(range(KC))
        N_FIRST, N_X, N_TOP = 5, 3, 5
        block = ctx.enter_context(nc.Block())

        @block.sync
        def _(sp):
            sp.dma_start(ids[:], a["ids"].rearrange("(t g s) f -> g t (s f)", g=128, s=SQ)).then_inc(ids_in, 16)
            sp.dma_start(eye[:], a["eye"]).then_inc(eye_in, 16)
            sp.dma_start(row_base[:], a["row_base"]).then_inc(base_in, 16)
            sp.dma_start(ws[:], a["Ws"]).then_inc(first_in, 16)
            sp.dma_start(centre[:], a["centre"]).then_inc(first_in, 16)
            sp.dma_start(gs_bs[:], a["gs_bs"]).then_inc(first_in, 16)
            sp.dma_start(wsi[:], a["Wsi_blocks"]).then_inc(first_in, 16)
            sp.dma_start(last_one[:], a["last_one"]).then_inc(first_in, 16)

            sp.dma_start(pair_gb[:], a["pair_gb"]).then_inc(fold_in, 16)
            sp.dma_start(masks[:], a["masks"]).then_inc(fold_in, 16)
            sp.dma_start(w1z[:], a["W1"][0:USED, :].rearrange("(c p) m -> p c m", p=128)).then_inc(w1z_in, 16)
            sp.dma_start(gl_bl[:], a["gl_bl"]).then_inc(w1z_in, 16)
            sp.dma_start(wl[:], a["Wl_rows"].rearrange("(c p) m -> p c m", p=128)).then_inc(wl_in, 16)

            dense = a["dense"].rearrange("(n g s) d -> n s g d", g=GB, s=SQ)

            def load_dense(i):
                for s in range(SQ):
                    sp.dma_start(dense_x[32 * s:32 * s + 32, :], dense[i, s]).then_inc(dense_x_in, 16)

            def body(i, n):
                units, layer, top = stages(n)
                for j in range(UB):
                    if j == 2 and n < NB - 1:
                        sp.wait_ge(dt_put, i + 1)
                        load_dense(i + 1)
                    if present(n, j)[2]:
                        of, quarter = (i - 1 if j < 2 else i), (j - 2) % UB
                        sp.wait_ge(zs_ready, UB * i + j - 1)
                        sp.dma_start(scratch[of, :, GU * quarter:GU * quarter + GU, :],
                                     zs[:, j % 2]).then_inc(z_stored[j % 2], 16)
                    if j == 1 and layer:
                        for m in range(2):
                            sp.wait_ge(z_stored[m], 32 * i)
                        sp.sem_inc(read_begun, 1)
                        for s in range(SQ):
                            sp.dma_start(plain[32 * s:32 * s + 32],
                                         scratch[i - 1, 32 * s:32 * s + 32, :, :].rearrange("p g c -> g p c")
                                         ).then_inc(zb_in, 16)

            load_dense(0)
            sp.dma_start(wd[:], a["WdT"].rearrange("(c p) e -> p c e", p=128)).then_inc(x_weights_in, 16)
            sp.dma_start(gd_b[:], a["gd_rows"]).then_inc(x_weights_in, 16)
            sp.dma_start(bd_b[:], a["bd_rows"]).then_inc(x_weights_in, 16)
            sp.wait_ge(et_put, 1)
            sp.dma_start(b1[:], a["b1"]).then_inc(top_weights_in, 16)
            sp.dma_start(w1[:, 3:5, :], a["W1"][ML:ML + DD, :].rearrange("(c p) m -> p c m", p=128)
                         ).then_inc(top_weights_in, 16)
            sp.dma_start(w2[:], a["W2"].rearrange("(c p) m -> p c m", p=128)).then_inc(top_weights_in, 16)
            sp.dma_start(b2[:], a["b2"]).then_inc(top_weights_in, 16)
            sp.dma_start(w3[:], a["W3"]).then_inc(top_weights_in, 16)
            iterations(sp, body, peel=True)
            sp.wait_ge(out_ready, NB)
            sp.dma_start(a["out"].rearrange("(a b) c -> a (b c)", a=1),
                         y_row[:].rearrange("p n g s -> p (n g s)")).then_inc(out_stored, 16)
            sp.wait_ge(out_stored, 16)

        @block.gpsimd
        def _(pool):
            def body(i):
                for j in range(UB):
                    pool.wait_ge(index_ready, UB * i + j + 1)
                    pool.sem_inc(gather_begun, 1)
                    for g in range(GU):
                        pool.indirect_dma_start(
                            out=rows[:, j, g, :], out_offset=None, in_=a["table"],
                            in_offset=bass.IndirectOffsetOnAxis(ap=index_now[:, j, g:g + 1], axis=0),
                        ).then_inc(gathered[j], 16)
            body(0)
            with pool.Fori(1, NB) as i:
                body(i)

        @block.tensor
        def _(pe):
            pe.wait_ge(eye_in, 16)
            pe.wait_ge(ids_float, 1)
            nc.tensor.transpose(p_z[0:ROWS, 0:128], ids_f[:, 0, :], eye[:]).then_inc(ids_turned, 1)
            pe.wait_ge(ids_float, 2)
            for t in range(1, 4):
                last = nc.tensor.transpose(p_a[0:ROWS, 128 * t:128 * t + 128], ids_f[:, t, :], eye[:])
            last.then_inc(ids_turned, 1)
            pe.wait_ge(first_in, 16 * N_FIRST)
            nc.tensor.matmul(p_b[:, 0:D], centre[:], ws[:], start=True, stop=True).then_inc(wc_done, 1)
            pe.wait_ge(wc_ready, 2)
            nc.tensor.transpose(p_t[0:D + 1, 0:E], wc_gs[:], eye[:])
            nc.tensor.matmul(p_q[0:D, 0:D], wc[:], wc[:], start=True, stop=True)
            nc.tensor.matmul(p_q[D:2 * D, 0:D], wc[:], wc[:], start=True, stop=True).then_inc(wy_done, 1)
            pe.wait_ge(wsi_ready, 1)
            nc.tensor.matmul(p_u[0:D + 1, 0:SQ * NP], last_one[:], wsi_c[:].rearrange("r s p -> r (s p)"),
                             start=True, stop=True).then_inc(u_const_done, 1)
            pe.wait_ge(units_ready, 1)

            def body(i, n):
                units, layer, top = stages(n)
                for j in range(UB):
                    k = UB * i + j
                    now, lag1, lag2 = present(n, j)
                    if now:
                        pe.wait_ge(gathered[j], 16 * GU * (i + 1))
                        after(pe, et_ready, k)
                        for m in range(GU // 2):
                            last = nc.tensor.transpose(
                                p_t[:, ROWS * m:ROWS * m + ROWS],
                                rows[:, j, 2 * m:2 * m + 2, :].rearrange("r g d -> r (g d)"), eye[0:ROWS, 0:ROWS])
                        last.then_inc(et_put, 1)
                    if j == 0 and units:
                        after(pe, zt_low_ready, 2 * (i - 1))
                        pe.wait_ge(dense_x_in, 64 * (i + 1))
                        for c in range(2):
                            last = nc.tensor.transpose(p_a[:, 128 * c:128 * c + 128],
                                                       dense_x[:, 128 * c:128 * c + 128], eye[:])
                        last.then_inc(dt_put, 1)
                    if lag1:
                        pe.wait_ge(rows_ready, k)
                        after(pe, ut_ready, 2 * (k - 1))
                        for g in range(GU // 2):
                            for h in range(2):
                                last = nc.tensor.matmul(p_u[D * h:D * h + D, 128 * g:128 * g + 128],
                                                        rows_n[:, GU // 2 * h + g, :],
                                                        wsi_c[:].rearrange("r s p -> r (s p)"), start=True, stop=True)
                        last.then_inc(u_done, 1)
                    if now:
                        pe.wait_ge(et_ready, k + 1)
                        after(pe, q_used, k)
                        for m in range(GU // 2):
                            last = nc.tensor.matmul(p_q[0:ROWS, 128 * m:128 * m + 128], et[:, m, :], gram[:],
                                                    start=True, stop=True)
                        last.then_inc(q_done, 1)
                    if j == 0 and top:
                        pe.wait_ge(z_hat_ready, i - 1)
                        for c in range(3):
                            last = nc.tensor.transpose(p_b[:, 128 * c:128 * c + 128],
                                                       z_hat[:, 128 * c:128 * c + 128], eye[:])
                        last.then_inc(hz_done, 1)
                    if j == 2 and units:
                        pe.wait_ge(x_ready, i + 1)
                        nc.tensor.transpose(p_a[:, 128:256], x_full[:], eye[:]).then_inc(xt_done, 1)
                    if j == 3 and top:
                        pe.wait_ge(h2_ready, 2 * (i - 1))
                        for c in range(2):
                            last = nc.tensor.matmul(p_b[0:1, 256:384], w3[:, c:c + 1], h2[:, c, :],
                                                    start=c == 0, stop=c == 1)
                        last.then_inc(out_done, 1)
                    if j == 3 and layer:
                        if n == 1:
                            pe.wait_ge(wk_summed, 1)
                        pe.wait_ge(zb_in, 64 * i)
                        if units:
                            pe.wait_ge(xt_ready, i + 1)
                        for k4 in range(16):
                            q = k4 % 4
                            last = nc.tensor.matmul(p_a[32 * q:32 * q + 32, 32 * (k4 - q):32 * (k4 - q) + 128],
                                                    skew[:, :, k4], eye[:], start=True, stop=True)
                        last.then_inc(zt_done, 1)
                        pe.wait_ge(sum_put, i)
                        after(pe, out_ready, i - 1)
                        for q, products in enumerate((skew[:, :, 16], skew[:, :, 17], plain[:, :, 1], plain[:, :, 0])):
                            last = nc.tensor.matmul(p_b[32 * q:32 * q + 32, PACK:PACK + 128], products, eye[:],
                                                    start=True, stop=True)
                        last.then_inc(pack_done, 1)
                    if lag1:
                        after(pe, y_ready, k - 1)
                        for h in range(2):
                            pe.wait_ge(ut_ready, 2 * k - 1 + h)
                            last = nc.tensor.matmul(p_y[:, 512 * h:512 * h + 512], wy[:],
                                                    ut[:, 4 * h:4 * h + 4, :].rearrange("d g c -> d (g c)"),
                                                    start=True, stop=True)
                        last.then_inc(y_done, 1)
                    if j == 0 and units:
                        pe.wait_ge(dt_ready, 2 * (i + 1))
                        pe.wait_ge(x_weights_in, 16 * N_X)
                        for c in range(2):
                            last = nc.tensor.matmul(p_a[:, 0:E], dt[:, c, :], wd[:, c, :], start=c == 0, stop=c == 1)
                        last.then_inc(x_done, 1)
                    if lag2:
                        pe.wait_ge(y_ready, k - 1)
                        pe.wait_ge(xt_ready, i if j < 2 else i + 1)
                        if n == 0 and j == 2:
                            pe.wait_ge(bl_ready, 1)
                        after(pe, zs_ready, k - 2)
                        for g in range(GU):
                            for s in range(SQ):
                                f = feat[:, (j - 2) % UB, SQ * g + s, :]
                                last = nc.tensor.matmul(p_z[32 * s:32 * s + 32, SLOTS * g:SLOTS * g + SLOTS],
                                                        f[:, 2:SLOTS], f, start=True, stop=True)
                        last.then_inc(z_done, 1)
                    if n == 0 and j >= 1:
                        if j == 1:
                            pe.wait_ge(wl_in, 16)
                            pe.wait_ge(fold_ready, 1)
                        for c in FOLD[j - 1]:
                            last = nc.tensor.matmul(p_b[:], fold[:, c, :], wl[:, c, :], start=c == 0, stop=c == KC - 1)
                        if j == 3:
                            last.then_inc(fold_done, 1)
                    if n == 0 and j == 0:
                        pe.wait_ge(w1z_in, 32)
                        for m in range(4):
                            for c in range(3):
                                last = nc.tensor.matmul(p_z[:, m:m + 1], w1z[:, c, 128 * m:128 * m + 128],
                                                        gl_bl[:, 1, c:c + 1], start=c == 0, stop=c == 2)
                        last.then_inc(bl_done, 1)
                    if j == 0 and top:
                        pe.wait_ge(dt_ready, 2 * (i - 1))
                        pe.wait_ge(hz_ready, i - 1)
                        for m in range(CUT[n == NB]):
                            for c in range(5):
                                nc.tensor.matmul(p_b[:, 128 * m:128 * m + 128], w1[:, c, 128 * m:128 * m + 128],
                                                 hz[:, c, :] if c < 3 else dt_all[:, i - 2, c - 3, :],
                                                 start=c == 0, stop=c == 4)
                    if j == 1 and top:
                        for m in range(CUT[n == NB], 4):
                            for c in range(5):
                                last = nc.tensor.matmul(p_b[:, 128 * m:128 * m + 128],
                                                        w1[:, c, 128 * m:128 * m + 128],
                                                        hz[:, c, :] if c < 3 else dt_all[:, i - 2, c - 3, :],
                                                        start=c == 0, stop=c == 4)
                        last.then_inc(h1_done, 1)
                    if j == 2 and top:
                        pe.wait_ge(h1_ready, 4 * (i - 1))
                        for m in range(2):
                            for c in range(4):
                                last = nc.tensor.matmul(p_b[:, 128 * m:128 * m + 128],
                                                        w2[:, c, 128 * m:128 * m + 128], h1[:, c, :],
                                                        start=c == 0, stop=c == 3)
                        last.then_inc(h2_done, 1)
                    if j == 3 and layer:
                        pe.wait_ge(zt_ready, i)
                        pe.wait_ge(zt_low_ready, 2 * i - 1)
                        if n == 1:
                            pe.wait_ge(top_ready, 1)
                        for c in range(KC):
                            nc.tensor.matmul(p_b[:], zt_high[:, c, :], wk_low[:, c, :], start=c == 0, stop=False)
                        for c in range(KC):
                            nc.tensor.matmul(p_b[:], zt_high[:, c, :], wk_high[:, c, :], start=False, stop=False)
                        pe.wait_ge(zt_low_ready, 2 * i)
                        for c in range(KC):
                            last = nc.tensor.matmul(p_b[:], zt_low[:, c, :], wk_high[:, c, :], start=False,
                                                    stop=c == KC - 1)
                        last.then_inc(l_done, 1)

            iterations(pe, body)

        @block.scalar
        def _(act):
            act.wait_ge(units_ready, 1)
            nc.scalar.activation(x_sd[:], eps_col[:], ACT.Sqrt).then_inc(table_loaded, 1)
            act.wait_ge(table_loaded, 1)

            def body(i, n):
                units, layer, top = stages(n)
                for j in range(UB):
                    k = UB * i + j
                    now, lag1, lag2 = present(n, j)
                    if j == 3 and top:
                        act.wait_ge(h2_done, i - 1)
                        after(act, out_done, i - 2)
                        for m in range(2):
                            nc.scalar.activation(h2[:, m, :], p_b[:, 128 * m:128 * m + 128], ACT.Relu,
                                                 bias=b2[:, m:m + 1]).then_inc(h2_ready, 1)
                    if now:
                        act.wait_ge(et_put, k + 1)
                        after(act, q_done, k)
                        nc.scalar.copy(et[:].rearrange("d m r -> d (m r)"), p_t[:, 0:ROWS * GU // 2]).then_inc(et_ready, 1)
                    if j == 0 and top:
                        act.wait_ge(l_var_ready, i - 1)
                        nc.scalar.activation(l_sd[:], l_mv[:, 1:2], ACT.Sqrt, bias=eps_col[:]).then_inc(l_sd_ready, 1)
                    if lag1:
                        act.wait_ge(u_done, k)
                        after(act, y_done, k - 1)
                        for h in range(2):
                            nc.scalar.copy(ut[0:D, GU // 2 * h:GU // 2 * (h + 1), :].rearrange("d g c -> d (g c)"),
                                           p_u[D * h:D * h + D, :]).then_inc(ut_ready, 1)
                    if j == 0 and units:
                        act.wait_ge(dt_put, i + 1)
                        after(act, x_done, i)
                        nc.scalar.copy(dt[:].rearrange("d c b -> d (c b)"), p_a[:, 0:DD]).then_inc(dt_ready, 1)
                        nc.scalar.copy(dt_all[:, i].rearrange("d c b -> d (c b)"), p_a[:, 0:DD]).then_inc(dt_ready, 1)
                    if j == 0 and top:
                        act.wait_ge(hz_done, i - 1)
                        nc.scalar.copy(hz[:].rearrange("d c b -> d (c b)"), p_b[:, 0:USED]).then_inc(hz_ready, 1)
                    if j == 2 and units:
                        act.wait_ge(xt_done, i + 1)
                        after(act, z_done, UB * i)
                        nc.scalar.copy(feat[:].rearrange("e u (g s) c -> e c s (u g)", s=SQ)[:, 0],
                                       p_a[:, 128:256].rearrange("e (s g) -> e s g", s=SQ)).then_inc(xt_ready, 1)
                    if j == 2 and top:
                        act.wait_ge(h1_done, i - 1)
                        after(act, h2_done, i - 2)
                        for m in range(4):
                            nc.scalar.activation(h1[:, m, :], p_b[:, 128 * m:128 * m + 128], ACT.Relu,
                                                 bias=b1z[:, m:m + 1]).then_inc(h1_ready, 1)
                    if j == 3 and top:
                        act.wait_ge(out_done, i - 1)
                        nc.scalar.copy(y_row[:, i - 2, :, :].rearrange("p g s -> p s g"),
                                       p_b[0:1, 256:384].rearrange("p (s g) -> p s g", s=SQ)).then_inc(out_ready, 1)
                    if now:
                        act.wait_ge(var_ready, k + 1)
                        nc.scalar.activation(sd_e[:], var_g[:], ACT.Sqrt).then_inc(sd_ready, 1)
                    if j == 3 and layer:
                        act.wait_ge(zt_done, i)
                        after(act, l_done, i - 1)
                        nc.scalar.copy(zt_high[:, 0:4, :].rearrange("r c b -> r (c b)"), p_a[:]).then_inc(zt_ready, 1)
                    if lag1:
                        act.wait_ge(y_done, k)
                        after(act, y_summed, k - 1)
                        nc.scalar.activation(y_sq[:].rearrange("e b p -> e (b p)"), p_y[:], ACT.Square).then_inc(sq_ready, 1)
                    if lag2:
                        act.wait_ge(z_done, k - 1)
                        after(act, z_stored[j % 2], 16 * (2 * i + (j - 2) // 2))
                        nc.scalar.copy(zs[:, j % 2].rearrange("r g c -> r (g c)"), p_z[:, 0:GU * SLOTS]).then_inc(zs_ready, 1)
                    if lag1:
                        act.wait_ge(y_summed, k)
                        nc.scalar.activation(y_sd[:], y_sum[:], ACT.Sqrt, bias=eps_col[:], scale=1.0 / NP).then_inc(y_sd_ready, 1)
                    if j == 0 and units:
                        act.wait_ge(x_var_ready, i + 1)
                        nc.scalar.activation(x_sd[:], x_mv[:, 1:2], ACT.Sqrt, bias=eps_col[:]).then_inc(x_sd_ready, 1)
                    if n == 1 and j == 3:
                        act.wait_ge(top_ready, 1)
                    if (n, j) in ((0, 3), (1, 1)):
                        if n == 1:
                            act.wait_ge(wk_summed, 1)
                        for c in range(KC - 1) if n == 0 else (KC - 1,):
                            act.wait_ge(wk_ready, c + 1)
                            nc.scalar.copy(wk_high[:, c, :], wk[:, c, :]).then_inc(wk_high_ready, 1)

            iterations(act, body)

        @block.vector
        def _(dve):
            dve.wait_ge(ids_in, 16)
            nc.vector.tensor_copy(ids_f[:, 0], ids[:, 0]).then_inc(ids_float, 1)
            nc.vector.tensor_copy(ids_f[:, 1:4], ids[:, 1:4]).then_inc(ids_float, 1)
            dve.wait_ge(base_in, 16)
            dve.wait_ge(ids_turned, 1)
            nc.vector.tensor_scalar(index_now[:].rearrange("r j g -> r (j g)"), p_z[0:ROWS, 0:UB * GU], row_base[:], None,
                                    ALU.add).then_inc(index_ready, UB)
            nc.vector.tensor_scalar(index[:, 0:128], p_z[0:ROWS, 0:128], row_base[:], None, ALU.add).then_inc(prepared, 1)
            nc.vector.memset(index[:, NG:], 0).then_inc(prepared, 1)
            nc.vector.memset(eps_col[:], EPS).then_inc(prepared, 1)
            nc.vector.memset(gram[:], 0.0).then_inc(prepared, 1)
            dve.wait_ge(ids_turned, 2)
            nc.vector.tensor_scalar(index[:, 128:NG], p_a[0:ROWS, 128:NG], row_base[:], None, ALU.add).then_inc(prepared, 1)
            dve.wait_ge(wc_done, 1)
            nc.vector.tensor_copy(wc[:], p_b[:, 0:D]).then_inc(wc_ready, 1)
            nc.vector.tensor_copy(wc_gs[:, D:D + 1], gs_bs[:, 1:2]).then_inc(prepared, 1)
            dve.wait_ge(prepared, 6)
            nc.vector.tensor_scalar(wc_gs[:, 0:D], p_b[:, 0:D], gs_bs[:, 0:1], None, ALU.mult).then_inc(wc_ready, 1)
            nc.vector.tensor_reduce(wsi_sum[:], wsi[:], AX, ALU.add).then_inc(prepared, 1)
            dve.wait_ge(prepared, 7)
            nc.vector.scalar_tensor_tensor(out=wsi_c[:], in0=wsi_sum[:].unsqueeze(2).to_broadcast([ROWS, SQ, NP]),
                                           scalar=-1.0 / NP, in1=wsi[:], op0=ALU.mult, op1=ALU.add).then_inc(wsi_ready, 1)
            nc.vector.memset(feat[:, :, :, 1], 1.0).then_inc(prepared, 1)
            nc.vector.memset(zb[:], 0.0).then_inc(prepared, 1)
            dve.wait_ge(wy_done, 1)
            nc.vector.tensor_copy(wy[:], p_t[0:D + 1, 0:E]).then_inc(prepared, 1)
            for h in range(2):
                nc.vector.tensor_scalar(gram[D * h:D * h + D, D * h:D * h + D], p_q[D * h:D * h + D, 0:D], 1.0 / E,
                                        None, ALU.mult).then_inc(prepared, 1)
            dve.wait_ge(u_const_done, 1)
            nc.vector.tensor_copy(ut[D:D + 1, :, :], p_u[D:D + 1, 0:SQ * NP].unsqueeze(1).to_broadcast([1, GU, SQ * NP])
                                  ).then_inc(prepared, 1)
            dve.wait_ge(prepared, 13)
            nc.vector.sem_inc(units_ready, 1)

            dve.wait_ge(fold_in, 32)
            for n, (u, v) in enumerate(((0, 1), (0, 3), (1, 2), (2, 3))):
                nc.vector.tensor_tensor(pair_x[:, n, :], pair_gb[:, u, :], pair_gb[:, v, :], ALU.mult).then_inc(prepared, 1)
            dve.wait_ge(prepared, 17)
            for c in range(KC):
                nc.vector.tensor_scalar(fold[:, c, :], masks[:, 0, c, :], pair_x[:, 1, c:c + 1], None, ALU.mult
                                        ).then_inc(prepared, 1)
            for m in (1, 2):
                dve.wait_ge(prepared, 17 + KC * m)
                for c in range(KC):
                    nc.vector.scalar_tensor_tensor(
                        out=fold[:, c, :], in0=masks[:, m, c, :], scalar=pair_x[:, m + 1, c:c + 1],
                        in1=fold[:, c, :], op0=ALU.mult, op1=ALU.add).then_inc(prepared, 1)
            dve.wait_ge(prepared, 32)
            nc.vector.sem_inc(fold_ready, 1)
            nc.vector.memset(skew[:, NP - 1:NP, 17], 1.0).then_inc(prepared, 1)

            def lower(chunks):
                for c in chunks:
                    dve.wait_ge(wk_high_ready, c + 1)
                    nc.vector.tensor_tensor(wk_low[:, c, :], wk[:, c, :], wk_high[:, c, :].bitcast(F32), ALU.subtract
                                            ).then_inc(prepared, 1)

            def prepare_layers(part):
                if part == 0:
                    dve.wait_ge(bl_done, 1)
                    nc.vector.tensor_copy(bl_w1[:], p_z[:, 0:4]).then_inc(bl_ready, 1)
                    dve.wait_ge(w1z_in, 32)
                    for c in range(3):
                        nc.vector.tensor_scalar(w1[:, c, :], w1z[:, c, :], gl_bl[:, 0, c:c + 1], None, ALU.mult
                                                ).then_inc(prepared, 1)
                elif part == 1:
                    dve.wait_ge(wl_in, 16)
                    for c in range(KC):
                        nc.vector.tensor_scalar(wk[:, c, :], wl[:, c, :], pair_x[:, 0, c:c + 1], None, ALU.mult
                                                ).then_inc(wk_ready, 1)
                elif part == 2:
                    dve.wait_ge(fold_done, 1)
                    dve.wait_ge(wk_ready, KC)
                    nc.vector.tensor_tensor(wk[:, KC - 1, :], wk[:, KC - 1, :], p_b[:], ALU.add).then_inc(wk_summed, 1)
                    lower((0, 1))
                elif part == 3:
                    lower((2, 3))
                    dve.wait_ge(top_weights_in, 16 * N_TOP)
                    dve.wait_ge(bl_ready, 1)
                    nc.vector.tensor_tensor(b1z[:], bl_w1[:], b1[:], ALU.add).then_inc(prepared, 1)
                else:
                    lower((4,))
                    dve.wait_ge(prepared, 42)
                    nc.vector.sem_inc(top_ready, 1)

            def body(i, n):
                units, layer, top = stages(n)
                for j in range(UB):
                    k = UB * i + j
                    now, lag1, _ = present(n, j)
                    if j == 0 and top:
                        dve.wait_ge(l_done, i - 1)
                        nc.vector.bn_stats(l_stat[:], p_b[:]).then_inc(l_stat_ready, 1)
                        dve.wait_ge(top_weights_in, 16 * N_TOP)
                        dve.wait_ge(l_stat_ready, i - 1)
                        nc.vector.bn_aggr(l_mv[:], l_stat[:]).then_inc(l_var_ready, 1)
                        dve.wait_ge(l_sd_ready, i - 1)
                        nc.vector.reciprocal(l_rs[:], l_sd[:]).then_inc(l_rs_ready, 1)
                        dve.wait_ge(l_rs_ready, i - 1)
                        nc.vector.tensor_scalar(z_hat[:], p_b[:, 0:USED], l_mv[:, 0:1], l_rs[:], ALU.subtract, ALU.mult
                                                ).then_inc(z_hat_ready, 1)
                    if now:
                        dve.wait_ge(q_done, k + 1)
                        nc.vector.tensor_tensor(prod[:].rearrange("r g d -> r (g d)"), p_q[0:ROWS, :],
                                                rows[:, j, :, :].rearrange("r g d -> r (g d)"), ALU.mult).then_inc(q_used, 1)
                        dve.wait_ge(q_used, k + 1)
                        nc.vector.tensor_reduce(var_e[:], prod[:], AX, ALU.add).then_inc(var_summed, 1)
                        dve.wait_ge(var_summed, k + 1)
                        nc.vector.tensor_scalar(var_g[:], var_e[:], 0.0, EPS, ALU.max, ALU.add).then_inc(var_ready, 1)
                        dve.wait_ge(sd_ready, k + 1)
                        nc.vector.reciprocal(rs_e[:], sd_e[:]).then_inc(rs_ready, 1)
                        dve.wait_ge(rs_ready, k + 1)
                        after(dve, u_done, k)
                        nc.vector.tensor_tensor(rows_n[:], rows[:, j, :, :], rs_e[:].unsqueeze(2).to_broadcast([ROWS, GU, D]),
                                                ALU.mult).then_inc(rows_ready, 1)
                        nc.vector.tensor_copy(index_now[:, j, :], index[:, bass.ds(GU * (k + UB), GU)]).then_inc(index_ready, 1)
                    if j == 3 and layer:
                        dve.wait_ge(pack_done, i)
                        after(dve, l_done, i - 1)
                        nc.vector.tensor_copy(zt_high[:, KC - 1, :], p_b[:, PACK:PACK + 128]).then_inc(pack_ready, 1)
                        dve.wait_ge(pack_ready, i)
                        nc.vector.tensor_tensor(zt_low[:, KC - 1, :], p_b[:, PACK:PACK + 128],
                                                zt_high[:, KC - 1, :].bitcast(F32), ALU.subtract).then_inc(zt_low_ready, 1)
                        dve.wait_ge(zt_ready, i)
                        nc.vector.tensor_tensor(zt_low[:, 0:KC - 1, :].rearrange("r c b -> r (c b)"), p_a[:],
                                                zt_high[:, 0:KC - 1, :].rearrange("r c b -> r (c b)").bitcast(F32),
                                                ALU.subtract).then_inc(zt_low_ready, 1)
                    if lag1:
                        dve.wait_ge(sq_ready, k)
                        nc.vector.tensor_reduce(y_sum[:], y_sq[:], AX, ALU.add).then_inc(y_summed, 1)
                    if j == 0 and units:
                        dve.wait_ge(x_done, i + 1)
                        nc.vector.bn_stats(x_stat[:], p_a[:, 0:E]).then_inc(x_chain, 1)
                        dve.wait_ge(x_weights_in, 16 * N_X)
                        dve.wait_ge(x_chain, 4 * i + 1)
                        nc.vector.bn_aggr(x_mv[:], x_stat[:]).then_inc(x_var_ready, 1)
                    if lag1:
                        dve.wait_ge(y_sd_ready, k)
                        nc.vector.reciprocal(y_rs[:], y_sd[:]).then_inc(y_rs_ready, 1)
                        dve.wait_ge(y_rs_ready, k)
                        after(dve, z_done, k - UB)
                        nc.vector.tensor_tensor(feat[:, (j - 1) % UB, :, 2:SLOTS], p_y[:].rearrange("e (b p) -> e b p", p=NP),
                                                y_rs[:].unsqueeze(2).to_broadcast([E, SU, NP]), ALU.mult).then_inc(y_ready, 1)
                    if j == 0 and units:
                        dve.wait_ge(x_sd_ready, i + 1)
                        nc.vector.reciprocal(x_rs[:], x_sd[:]).then_inc(x_chain, 1)
                        dve.wait_ge(x_chain, 4 * i + 2)
                        nc.vector.tensor_scalar(x_hat[:], p_a[:, 0:E], x_mv[:, 0:1], x_rs[:], ALU.subtract, ALU.mult
                                                ).then_inc(x_chain, 1)
                        dve.wait_ge(x_chain, 4 * i + 3)
                        nc.vector.tensor_tensor(x_g[:], x_hat[:], gd_b[:], ALU.mult).then_inc(x_chain, 1)
                        dve.wait_ge(x_chain, 4 * i + 4)
                        nc.vector.tensor_tensor(x_full[:], x_g[:], bd_b[:], ALU.add).then_inc(x_ready, 1)
                    if j == 3 and units:
                        after(dve, pack_done, i)
                        nc.vector.tensor_reduce(skew[:, NP - 1:NP, 16], x_full[:], AX, ALU.add).then_inc(sum_put, 1)
                    if (n, j) in PREPARATION:
                        prepare_layers(PREPARATION.index((n, j)))

            iterations(dve, body)


_TABLES = [f"tbl_{f}" for f in range(NF)]


def kernel(**inputs):
    import concourse.bacc as _bacc
    from concourse.bass_utils import run_bass_kernel_spmd as _run

    x = {k: np.asarray(v) for k, v in inputs.items()}
    pairs = interaction_rows()
    wl_cols = np.concatenate([x["L0_rec_Wl"].T, np.zeros((1, ML), np.float32)])
    first = np.array([r[1] for r in pairs]).reshape(KC, 128).T
    second = np.array([r[2] for r in pairs]).reshape(KC, 128).T
    gsi = np.concatenate([x["L0_rec_gsi"], np.array([1.0, 0.0], np.float32)])
    bsi = np.concatenate([x["L0_rec_bsi"], np.array([0.0, 0.0], np.float32)])
    wsi_blocks = np.zeros((SQ, NF, SQ, NP), np.float32)
    for s in range(SQ):
        wsi_blocks[s, :, s, :] = x["L0_rec_Wsi"].T
    masks = np.zeros((3, KC * 128, 128), np.float32)
    for n, (col, p, q) in enumerate(pairs):
        if col < 0:
            continue
        if q < NP:
            masks[0, n, COL_ONES + p] = 1.0
            masks[1, n, COL_ONES + q] = 1.0
            masks[2, n, COL_ONE] = float(E)
        else:
            masks[1, n, COL_SUM] = 1.0
    last_one = np.zeros((ROWS, D + 1), np.float32)
    last_one[:, D] = 1.0
    base = np.concatenate([[0], np.cumsum(VOCAB)[:-1]]).astype(np.float32)

    def cols(v):
        return v.reshape(-1, 128).T

    arrays = {
        "ids": x["ids"],
        "table": np.concatenate([x[t] for t in _TABLES]),
        "dense": x["r_dense_t"],
        "Ws": x["L0_rec_Ws"],
        "gs_bs": np.stack([x["L0_rec_gs"], x["L0_rec_bs"]], 1),
        "Wsi_blocks": wsi_blocks.reshape(ROWS, SQ, NP),
        "WdT": x["L0_rec_Wd"].T,
        "gd_rows": np.broadcast_to(x["L0_rec_gd"], (128, E)),
        "bd_rows": np.broadcast_to(x["L0_rec_bd"], (128, E)),
        "Wl_rows": wl_cols[[r[0] for r in pairs]],
        "pair_gb": np.stack([gsi[first], gsi[second], bsi[first], bsi[second]], 1),
        "W1": x["W_top1"],
        "gl_bl": np.stack([cols(x["L0_rec_gl"][:USED]), cols(x["L0_rec_bl"][:USED])], 1),
        "b1": cols(x["b_top1"]),
        "W2": x["W_top2"],
        "b2": cols(x["b_top2"]),
        "W3": x["W_top3"].reshape(2, 128).T,
        "eye": np.eye(128, dtype=np.float32),
        "centre": (np.eye(E) - 1.0 / E).astype(np.float32),
        "masks": masks.reshape(3, KC, 128, 128).transpose(2, 0, 1, 3),
        "last_one": last_one,
        "row_base": np.tile(base, SQ).reshape(ROWS, 1),
    }
    arrays = {k: np.ascontiguousarray(v) for k, v in arrays.items()}
    nc = _bacc.Bacc("TRN2", target_bir_lowering=False, num_devices=1)
    a = {k: nc.dram_tensor(f"in_{k}", v.shape, mybir.dt.from_np(v.dtype), kind="ExternalInput").ap()
         for k, v in arrays.items()}
    a["out"] = nc.dram_tensor("out_y", (B, 1), F32, kind="ExternalOutput").ap()
    dlrm_kernel(nc, a)
    r = _run(nc, [{f"in_{k}": v for k, v in arrays.items()}], core_ids=[0])
    return r.results[0]["out_y"]
```
